# Optimizing a Trainium2 kernel written in Bass

```python
import numpy as np
import jax
import jax.numpy as jnp

def _softmax(x, axis=-1):
    return jax.nn.softmax(x, axis=axis)

def _gelu(x):
    return jax.nn.gelu(x, approximate=True)

def _silu(x):
    return jax.nn.silu(x)

def _sigmoid(x):
    return jax.nn.sigmoid(x)

def _layernorm(x, axis=-1, eps=1e-05):
    m = jnp.mean(x, axis=axis, keepdims=True)
    v = jnp.var(x, axis=axis, keepdims=True)
    return (x - m) / jnp.sqrt(v + eps)

def _scatter_add(tgt, idx, src, axis=0):
    return tgt.at[idx].add(src)

def _segment_sum(src, seg, n):
    return jax.ops.segment_sum(src, seg, n)
kernel_name = 'mk_macaron_d2_jaxref_r8_610984'

def setup_inputs(seed: int=0):
    np.random.seed(seed)
    _w = jnp.asarray

    def _L0_attn_setup():
        import jax, jax.numpy as jnp
        import numpy as np
        DIM = 128
        N_HEADS = 16
        HEAD_DIM = DIM // N_HEADS

        def apply_rope(x):
            B, T, H, D = x.shape
            half = D // 2
            x1, x2 = (x[..., :half], x[..., half:])
            theta = 1.0 / 10000.0 ** (jnp.arange(0, half, 2, dtype=jnp.float32) / half)
            pos = jnp.arange(T, dtype=jnp.float32)
            freq = pos[:, None] * theta[None, :]
            sin = jnp.sin(freq)[None, :, None, :]
            cos = jnp.cos(freq)[None, :, None, :]
            x1e, x1o = (x1[..., ::2], x1[..., 1::2])
            x2e, x2o = (x2[..., ::2], x2[..., 1::2])
            x1r = jnp.concatenate([x1e * cos - x1o * sin, x1e * sin + x1o * cos], axis=-1)
            x2r = jnp.concatenate([x2e * cos - x2o * sin, x2e * sin + x2o * cos], axis=-1)
            return jnp.concatenate([x1r, x2r], axis=-1)
        key = jax.random.key(seed)
        ks = jax.random.split(key, 9)
        B, T, C, D = (2, 256, DIM, HEAD_DIM)
        s = 0.02
        return {'x': jax.random.normal(ks[0], (B, T, C), dtype=jnp.float32), 'Wq': jax.random.normal(ks[1], (C, C), dtype=jnp.float32) * s, 'bq': jnp.zeros((C,), dtype=jnp.float32), 'Wk': jax.random.normal(ks[2], (C, D), dtype=jnp.float32) * s, 'bk': jnp.zeros((D,), dtype=jnp.float32), 'Wv': jax.random.normal(ks[3], (C, D), dtype=jnp.float32) * s, 'bv': jnp.zeros((D,), dtype=jnp.float32), 'Wo': jax.random.normal(ks[4], (C, C), dtype=jnp.float32) * s, 'bo': jnp.zeros((C,), dtype=jnp.float32)}
    _L0_attn_in = _L0_attn_setup()

    def _L0_ffn_setup():
        import jax, jax.numpy as jnp
        import numpy as np
        D_MODEL = 128
        N_HEADS = 16
        N_EXPERTS = 8
        TOP_K = 2
        EXPERT_HIDDEN = D_MODEL * 4 // N_EXPERTS

        def layer_norm(x, g, b, eps=1e-05):
            mu = jnp.mean(x, axis=-1, keepdims=True)
            var = jnp.var(x, axis=-1, keepdims=True)
            return (x - mu) * jax.lax.rsqrt(var + eps) * g + b
        key = jax.random.key(seed)
        ks = jax.random.split(key, 12)
        s = 1.0 / np.sqrt(D_MODEL)
        return {'x': jax.random.normal(ks[0], (2, 256, D_MODEL), dtype=jnp.float32), 'Wq': jax.random.normal(ks[1], (D_MODEL, D_MODEL), dtype=jnp.float32) * s, 'Wk': jax.random.normal(ks[2], (D_MODEL, D_MODEL), dtype=jnp.float32) * s, 'Wv': jax.random.normal(ks[3], (D_MODEL, D_MODEL), dtype=jnp.float32) * s, 'Wo': jax.random.normal(ks[4], (D_MODEL, D_MODEL), dtype=jnp.float32) * s, 'g1': jnp.ones((D_MODEL,), jnp.float32), 'b1': jnp.zeros((D_MODEL,), jnp.float32), 'g2': jnp.ones((D_MODEL,), jnp.float32), 'b2': jnp.zeros((D_MODEL,), jnp.float32), 'Wg': jax.random.normal(ks[5], (D_MODEL, N_EXPERTS), dtype=jnp.float32) * s, 'W1': jax.random.normal(ks[6], (N_EXPERTS, D_MODEL, EXPERT_HIDDEN), dtype=jnp.float32) * s, 'W2': jax.random.normal(ks[7], (N_EXPERTS, EXPERT_HIDDEN, D_MODEL), dtype=jnp.float32) * (1.0 / np.sqrt(EXPERT_HIDDEN))}
    _L0_ffn_in = _L0_ffn_setup()

    def _L1_attn_setup():
        import jax, jax.numpy as jnp
        import numpy as np
        D_MODEL = 128
        NHEAD = 16
        HEAD_DIM = D_MODEL // NHEAD
        B, L = (4, 1024)
        LN_EPS = 1e-05

        def _decay_scan(v, lam):
            a = jnp.broadcast_to(lam[None, None, :, None], v.shape)

            def combine(c1, c2):
                a1, b1 = c1
                a2, b2 = c2
                return (a1 * a2, b1 * a2 + b2)
            _, state = jax.lax.associative_scan(combine, (a, v), axis=1)
            return state

        def _layernorm(y, gamma, beta):
            mu = jnp.mean(y, axis=-1, keepdims=True)
            var = jnp.mean(jnp.square(y - mu), axis=-1, keepdims=True)
            return (y - mu) * jax.lax.rsqrt(var + LN_EPS) * gamma + beta
        key = jax.random.key(seed)
        ks = jax.random.split(key, 8)
        s = 1.0 / np.sqrt(D_MODEL)
        return {'x': jax.random.normal(ks[0], (B, L, D_MODEL), dtype=jnp.float32), 'decay': jax.random.uniform(ks[1], (NHEAD,), dtype=jnp.float32, minval=0.8, maxval=0.999), 'Wq': jax.random.normal(ks[2], (D_MODEL, D_MODEL), dtype=jnp.float32) * s, 'Wv': jax.random.normal(ks[3], (D_MODEL, D_MODEL), dtype=jnp.float32) * s, 'Wg': jax.random.normal(ks[4], (D_MODEL, D_MODEL), dtype=jnp.float32) * s, 'Wo': jax.random.normal(ks[5], (D_MODEL, D_MODEL), dtype=jnp.float32) * s, 'ln_gamma': jnp.ones((D_MODEL,), dtype=jnp.float32), 'ln_beta': jnp.zeros((D_MODEL,), dtype=jnp.float32)}
    _L1_attn_in = _L1_attn_setup()

    def _L1_ffn_setup():
        import jax, jax.numpy as jnp
        import numpy as np
        B, S, H = (2, 128, 128)
        DFF = 256
        E = 8
        TOPK = 2

        def _expert_ffn(x, w1, b1, w2, b2, wg, bg, w3, b3):
            x1 = jnp.einsum('bsh,hf->bsf', x, w1) + b1
            x2 = jnp.einsum('bsh,hf->bsf', x, w2) + b2
            z = x1 * x2
            s = jax.nn.silu(jnp.einsum('bsf,fg->bsg', z, wg) + bg)
            return jnp.einsum('bsg,gh->bsh', s, w3) + b3
        key = jax.random.key(seed)
        ks = jax.random.split(key, 12)
        sc = 0.02
        return {'x': jax.random.normal(ks[0], (B, S, H), jnp.float32), 'gate_w': jax.random.normal(ks[1], (H, E), jnp.float32) * sc, 'gate_b': jnp.zeros((E,), jnp.float32), 'w1': jax.random.normal(ks[2], (E, H, DFF), jnp.float32) * sc, 'b1': jnp.zeros((E, DFF), jnp.float32), 'w2': jax.random.normal(ks[3], (E, H, DFF), jnp.float32) * sc, 'b2': jnp.zeros((E, DFF), jnp.float32), 'wg': jax.random.normal(ks[4], (E, DFF, DFF), jnp.float32) * sc, 'bg': jnp.zeros((E, DFF), jnp.float32), 'w3': jax.random.normal(ks[5], (E, DFF, H), jnp.float32) * sc, 'b3': jnp.zeros((E, H), jnp.float32)}
    _L1_ffn_in = _L1_ffn_setup()
    _d = {'L0_attn_x': _L0_attn_in['x'], 'L0_attn_Wq': _L0_attn_in['Wq'], 'L0_attn_bq': _L0_attn_in['bq'], 'L0_attn_Wk': _L0_attn_in['Wk'], 'L0_attn_bk': _L0_attn_in['bk'], 'L0_attn_Wv': _L0_attn_in['Wv'], 'L0_attn_bv': _L0_attn_in['bv'], 'L0_attn_Wo': _L0_attn_in['Wo'], 'L0_attn_bo': _L0_attn_in['bo'], 'L0_ffn_Wq': _L0_ffn_in['Wq'], 'L0_ffn_Wk': _L0_ffn_in['Wk'], 'L0_ffn_Wv': _L0_ffn_in['Wv'], 'L0_ffn_Wo': _L0_ffn_in['Wo'], 'L0_ffn_g1': _L0_ffn_in['g1'], 'L0_ffn_b1': _L0_ffn_in['b1'], 'L0_ffn_g2': _L0_ffn_in['g2'], 'L0_ffn_b2': _L0_ffn_in['b2'], 'L0_ffn_Wg': _L0_ffn_in['Wg'], 'L0_ffn_W1': _L0_ffn_in['W1'], 'L0_ffn_W2': _L0_ffn_in['W2'], 'L1_attn_decay': _L1_attn_in['decay'], 'L1_attn_Wq': _L1_attn_in['Wq'], 'L1_attn_Wv': _L1_attn_in['Wv'], 'L1_attn_Wg': _L1_attn_in['Wg'], 'L1_attn_Wo': _L1_attn_in['Wo'], 'L1_attn_ln_gamma': _L1_attn_in['ln_gamma'], 'L1_attn_ln_beta': _L1_attn_in['ln_beta'], 'L1_ffn_gate_w': _L1_ffn_in['gate_w'], 'L1_ffn_gate_b': _L1_ffn_in['gate_b'], 'L1_ffn_w1': _L1_ffn_in['w1'], 'L1_ffn_b1': _L1_ffn_in['b1'], 'L1_ffn_w2': _L1_ffn_in['w2'], 'L1_ffn_b2': _L1_ffn_in['b2'], 'L1_ffn_wg': _L1_ffn_in['wg'], 'L1_ffn_bg': _L1_ffn_in['bg'], 'L1_ffn_w3': _L1_ffn_in['w3'], 'L1_ffn_b3': _L1_ffn_in['b3']}
    _x0 = _d['L0_attn_x']
    _d['L0_attn_x'] = jax.random.normal(jax.random.fold_in(jax.random.key(seed), 1), (16, 256, 128), dtype=_x0.dtype)
    del _x0
    return _d

def reference(L0_attn_x, L0_attn_Wq, L0_attn_bq, L0_attn_Wk, L0_attn_bk, L0_attn_Wv, L0_attn_bv, L0_attn_Wo, L0_attn_bo, L0_ffn_Wq, L0_ffn_Wk, L0_ffn_Wv, L0_ffn_Wo, L0_ffn_g1, L0_ffn_b1, L0_ffn_g2, L0_ffn_b2, L0_ffn_Wg, L0_ffn_W1, L0_ffn_W2, L1_attn_decay, L1_attn_Wq, L1_attn_Wv, L1_attn_Wg, L1_attn_Wo, L1_attn_ln_gamma, L1_attn_ln_beta, L1_ffn_gate_w, L1_ffn_gate_b, L1_ffn_w1, L1_ffn_b1, L1_ffn_w2, L1_ffn_b2, L1_ffn_wg, L1_ffn_bg, L1_ffn_w3, L1_ffn_b3):

    def _L0_attn_ref(x, Wq, bq, Wk, bk, Wv, bv, Wo, bo):
        import jax, jax.numpy as jnp
        import numpy as np
        DIM = 128
        N_HEADS = 16
        HEAD_DIM = DIM // N_HEADS

        def apply_rope(x):
            B, T, H, D = x.shape
            half = D // 2
            x1, x2 = (x[..., :half], x[..., half:])
            theta = 1.0 / 10000.0 ** (jnp.arange(0, half, 2, dtype=jnp.float32) / half)
            pos = jnp.arange(T, dtype=jnp.float32)
            freq = pos[:, None] * theta[None, :]
            sin = jnp.sin(freq)[None, :, None, :]
            cos = jnp.cos(freq)[None, :, None, :]
            x1e, x1o = (x1[..., ::2], x1[..., 1::2])
            x2e, x2o = (x2[..., ::2], x2[..., 1::2])
            x1r = jnp.concatenate([x1e * cos - x1o * sin, x1e * sin + x1o * cos], axis=-1)
            x2r = jnp.concatenate([x2e * cos - x2o * sin, x2e * sin + x2o * cos], axis=-1)
            return jnp.concatenate([x1r, x2r], axis=-1)
        B, T, C = x.shape
        H, D = (N_HEADS, HEAD_DIM)
        q = (x @ Wq + bq).reshape(B, T, H, D).transpose(0, 2, 1, 3)
        k = x @ Wk + bk
        v = x @ Wv + bv
        q = apply_rope(q)
        k = apply_rope(k[:, None])[:, 0]
        scores = jnp.einsum('bhtd,bsd->bhts', q, k) / jnp.sqrt(jnp.float32(D))
        mask = jnp.tril(jnp.ones((T, T), dtype=bool))
        scores = jnp.where(mask[None, None], scores, -jnp.inf)
        probs = jax.nn.softmax(scores, axis=-1)
        attn = jnp.einsum('bhts,bsd->bhtd', probs, v)
        attn = attn.transpose(0, 2, 1, 3).reshape(B, T, C)
        return attn @ Wo + bo

    def _L0_ffn_ref(x, Wq, Wk, Wv, Wo, g1, b1, g2, b2, Wg, W1, W2):
        import jax, jax.numpy as jnp
        import numpy as np
        D_MODEL = 128
        N_HEADS = 16
        N_EXPERTS = 8
        TOP_K = 2
        EXPERT_HIDDEN = D_MODEL * 4 // N_EXPERTS

        def layer_norm(x, g, b, eps=1e-05):
            mu = jnp.mean(x, axis=-1, keepdims=True)
            var = jnp.var(x, axis=-1, keepdims=True)
            return (x - mu) * jax.lax.rsqrt(var + eps) * g + b
        B, S, D = x.shape
        H, dk = (N_HEADS, D // N_HEADS)
        xn = layer_norm(x, g1, b1)
        q = (xn @ Wq).reshape(B, S, H, dk).transpose(0, 2, 1, 3)
        k = (xn @ Wk).reshape(B, S, H, dk).transpose(0, 2, 1, 3)
        v = (xn @ Wv).reshape(B, S, H, dk).transpose(0, 2, 1, 3)
        scores = jnp.einsum('bhqd,bhkd->bhqk', q, k) / np.sqrt(dk)
        attn = jax.nn.softmax(scores, axis=-1)
        o = jnp.einsum('bhqk,bhkd->bhqd', attn, v)
        o = o.transpose(0, 2, 1, 3).reshape(B, S, D) @ Wo
        x = x + o
        xn2 = layer_norm(x, g2, b2)
        xf = xn2.reshape(B * S, D)
        gate = xf @ Wg
        topv, topi = jax.lax.top_k(gate, TOP_K)
        probs = jax.nn.softmax(topv, axis=-1)
        cw = jnp.sum(jax.nn.one_hot(topi, N_EXPERTS, dtype=xf.dtype) * probs[..., None], axis=1)
        h = jax.nn.relu(jnp.einsum('td,edh->teh', xf, W1))
        y = jnp.einsum('teh,ehd->ted', h, W2)
        moe = jnp.einsum('ted,te->td', y, cw).reshape(B, S, D)
        return x + moe

    def _L1_attn_ref(x, decay, Wq, Wv, Wg, Wo, ln_gamma, ln_beta):
        import jax, jax.numpy as jnp
        import numpy as np
        D_MODEL = 128
        NHEAD = 16
        HEAD_DIM = D_MODEL // NHEAD
        B, L = (4, 1024)
        LN_EPS = 1e-05

        def _decay_scan(v, lam):
            a = jnp.broadcast_to(lam[None, None, :, None], v.shape)

            def combine(c1, c2):
                a1, b1 = c1
                a2, b2 = c2
                return (a1 * a2, b1 * a2 + b2)
            _, state = jax.lax.associative_scan(combine, (a, v), axis=1)
            return state

        def _layernorm(y, gamma, beta):
            mu = jnp.mean(y, axis=-1, keepdims=True)
            var = jnp.mean(jnp.square(y - mu), axis=-1, keepdims=True)
            return (y - mu) * jax.lax.rsqrt(var + LN_EPS) * gamma + beta
        Bx, Lx, D = x.shape
        q = (x @ Wq.T).reshape(Bx, Lx, NHEAD, HEAD_DIM)
        v = (x @ Wv.T).reshape(Bx, Lx, NHEAD, HEAD_DIM)
        state = _decay_scan(v, decay)
        y = (q * state).reshape(Bx, Lx, D)
        y = _layernorm(y, ln_gamma, ln_beta)
        gate = jax.nn.silu(x @ Wg.T)
        y = y * gate
        return y @ Wo.T

    def _L1_ffn_ref(x, gate_w, gate_b, w1, b1, w2, b2, wg, bg, w3, b3):
        import jax, jax.numpy as jnp
        import numpy as np
        B, S, H = (2, 128, 128)
        DFF = 256
        E = 8
        TOPK = 2

        def _expert_ffn(x, w1, b1, w2, b2, wg, bg, w3, b3):
            x1 = jnp.einsum('bsh,hf->bsf', x, w1) + b1
            x2 = jnp.einsum('bsh,hf->bsf', x, w2) + b2
            z = x1 * x2
            s = jax.nn.silu(jnp.einsum('bsf,fg->bsg', z, wg) + bg)
            return jnp.einsum('bsg,gh->bsh', s, w3) + b3
        logits = jnp.einsum('bsh,he->bse', x, gate_w) + gate_b
        topv, topi = jax.lax.top_k(logits, TOPK)
        probs = jax.nn.softmax(topv, axis=-1)
        out = jnp.zeros_like(x)
        for e in range(E):
            we = jnp.sum(probs * (topi == e), axis=-1)
            y = _expert_ffn(x, w1[e], b1[e], w2[e], b2[e], wg[e], bg[e], w3[e], b3[e])
            out = out + we[..., None] * y
        return out
    x = L0_attn_x
    x = x + 0.5 * _L0_ffn_ref(_layernorm(x, axis=-1), L0_ffn_Wq, L0_ffn_Wk, L0_ffn_Wv, L0_ffn_Wo, L0_ffn_g1, L0_ffn_b1, L0_ffn_g2, L0_ffn_b2, L0_ffn_Wg, L0_ffn_W1, L0_ffn_W2)
    x = x + _L0_attn_ref(_layernorm(x, axis=-1), L0_attn_Wq, L0_attn_bq, L0_attn_Wk, L0_attn_bk, L0_attn_Wv, L0_attn_bv, L0_attn_Wo, L0_attn_bo)
    x = x + 0.5 * _L0_ffn_ref(_layernorm(x, axis=-1), L0_ffn_Wq, L0_ffn_Wk, L0_ffn_Wv, L0_ffn_Wo, L0_ffn_g1, L0_ffn_b1, L0_ffn_g2, L0_ffn_b2, L0_ffn_Wg, L0_ffn_W1, L0_ffn_W2)
    x = x + 0.5 * _L1_ffn_ref(_layernorm(x, axis=-1), L1_ffn_gate_w, L1_ffn_gate_b, L1_ffn_w1, L1_ffn_b1, L1_ffn_w2, L1_ffn_b2, L1_ffn_wg, L1_ffn_bg, L1_ffn_w3, L1_ffn_b3)
    x = x + _L1_attn_ref(_layernorm(x, axis=-1), L1_attn_decay, L1_attn_Wq, L1_attn_Wv, L1_attn_Wg, L1_attn_Wo, L1_attn_ln_gamma, L1_attn_ln_beta)
    x = x + 0.5 * _L1_ffn_ref(_layernorm(x, axis=-1), L1_ffn_gate_w, L1_ffn_gate_b, L1_ffn_w1, L1_ffn_b1, L1_ffn_w2, L1_ffn_b2, L1_ffn_wg, L1_ffn_bg, L1_ffn_w3, L1_ffn_b3)
    return x

_drawn_inputs = setup_inputs


def setup_inputs(seed=0):
    import zlib

    import numpy as np

    out = dict(_drawn_inputs(seed))
    spreads = {'L0_attn_bq': (0.0, 0.8),
     'L0_attn_bk': (0.0, 0.8),
     'L0_attn_bv': (0.0, 0.1),
     'L0_attn_bo': (0.0, 0.1),
     'L0_ffn_g1': (1.0, 0.2),
     'L0_ffn_b1': (0.0, 0.1),
     'L0_ffn_g2': (1.0, 0.2),
     'L0_ffn_b2': (0.0, 0.1),
     'L1_attn_ln_gamma': (1.0, 0.2),
     'L1_attn_ln_beta': (0.0, 0.285),
     'L1_ffn_gate_b': (0.0, 0.468),
     'L1_ffn_b1': (0.0, 0.8),
     'L1_ffn_b2': (0.0, 0.8),
     'L1_ffn_bg': (0.0, 0.8),
     'L1_ffn_b3': (0.0, 0.1)}
    factors = {'L0_attn_Wq': 8.0,
     'L0_attn_Wk': 8.0,
     'L0_attn_Wv': 4.509,
     'L1_ffn_w1': 8.0,
     'L1_ffn_w2': 8.0,
     'L1_ffn_wg': 8.0,
     'L1_ffn_w3': 8.0}
    for name, (base, spread) in spreads.items():
        noise = np.random.default_rng([zlib.crc32(name.encode()), seed]).standard_normal(out[name].shape)
        drawn = base * np.exp(spread * noise) if base else spread * noise
        out[name] = jnp.asarray(drawn.astype(out[name].dtype))
    for name, factor in factors.items():
        out[name] = (out[name] * factor).astype(out[name].dtype)
    return out
```

```python
from contextlib import ExitStack

import numpy as np
import concourse.bass as bass
from concourse import mybir

F32 = mybir.dt.float32
BF16 = mybir.dt.bfloat16
I32 = mybir.dt.int32
ALU = mybir.AluOpType
ACT = mybir.ActivationFunctionType
AX = mybir.AxisListType

P = 128
B, T = 16, 256
TILES = B * T // P
GT = 4
GROUPS = TILES // GT
GN = GT * P
H, D = 16, 8
QH = 4
QUADS = H // QH
E, K0 = 8, 64
CH = E * K0 // P
F1 = 256
TOKENS = B * T
SLOT_TILES = 2 * TOKENS // P + E
SLOTS = SLOT_TILES * P
RING = 8
ROW = P + 2
ARENA = 21500
NOWHERE = 1 << 20
EPS = 1e-5
SCALE = float(D) ** -0.5
MASKED = -1e30

PART_Q = [0, 1, 2, 0, 1, 0]
PART_K = [0, 0, 0, 1, 1, 2]
SPLIT_ROWS = D * len(PART_Q)
SHIFT_ROW = 96


def constants():
    ident = np.eye(P, dtype=np.float32)
    perm = np.zeros((D, D), np.float32)
    for out, src in enumerate([0, 2, 1, 3, 4, 6, 5, 7]):
        perm[out, src] = 1.0
    half = D // 2
    theta = (np.float32(1.0) / np.float32(10000.0) ** (np.arange(0, half, 2, dtype=np.float32) / np.float32(half)))
    rope = np.zeros((P, P), np.float32)
    for h in range(H):
        rot = np.zeros((D, D), np.float32)
        freq = (np.float32(h) * theta).astype(np.float32)
        for x in range(2):
            for n in range(2):
                even, odd = half * x + 2 * n, half * x + 2 * n + 1
                rot[half * x + n, even], rot[half * x + n, odd] = np.cos(freq[n]), -np.sin(freq[n])
                rot[half * x + 2 + n, even], rot[half * x + 2 + n, odd] = np.sin(freq[n]), np.cos(freq[n])
        rope[h * D:(h + 1) * D, h * D:(h + 1) * D] = rot.T @ perm
    key, query = np.arange(P)[:, None], np.arange(P)[None, :]
    mask_qk = np.where(query <= key, 0.0, MASKED).astype(np.float32)
    above = np.full((P, P), MASKED, np.float32)
    zero = np.zeros((P, P), np.float32)
    sel = np.zeros((P, CH * P), np.float32)
    for c in range(CH):
        for m in range(P):
            sel[(c * P + m) // K0, c * P + m] = 1.0
    before = (key < query).astype(np.float32)
    rev = np.tile(np.arange(E, 0, -1, dtype=np.float32), (P, 1))
    return {
        "ident": ident, "rope": rope,
        "mask_rows": np.concatenate([mask_qk, above, zero, mask_qk], 1),
        "mask_cols": np.concatenate([mask_qk.T, zero, above, mask_qk.T], 1),
        "sel": sel, "before": before, "rev": rev,
        "slot": np.tile(np.arange(SLOT_TILES, dtype=np.float32), (P, 1)),
        "token": (np.arange(TILES)[None, :] * P + np.arange(P)[:, None]).astype(np.float32),
    }


CONST = constants()
CONST_AT, _at = {}, 0
for _n, _a in CONST.items():
    CONST_AT[_n] = (_at, _a.shape[1])
    _at += _a.shape[1]
CONST_COLS = _at

COLS = ["f_g1", "f_b1", "f_g2", "f_b2", "a_bq", "a_bk", "s_gamma", "s_beta", "s_decay", "m_gate_b"]
ROWS = {"a_bv": P, "a_bo": P}
ROW_AT, _at = {}, 0
for _n, _w in ROWS.items():
    ROW_AT[_n] = (_at, _w)
    _at += _w
ROW_COLS = _at
MATS = ["f_Wq", "f_Wk", "f_Wv", "f_Wo", "a_WqT", "a_Wk", "a_Wv", "a_Wo", "s_WqT", "s_WvT", "s_WgT", "s_WoT"]


class Memory:

    def __init__(self, nc, ctx):
        self.nc, self.ctx = nc, ctx
        self.cst = self.keep("cst", [P, CONST_COLS])
        self.x = self.keep("x", [P, TILES, P])
        self.xi = self.keep("xi", [P, TILES, P])
        self.cols = self.keep("cols", [P, len(COLS)])
        self.rows = self.keep("rows", [P, ROW_COLS])
        self.mats = self.keep("mats", [P, len(MATS), P])
        self.identb = self.keep("identb", [P, P], BF16)
        self.maskb = self.keep("maskb", [P, 8, P], BF16)
        self.f_W1 = self.keep("f_W1", [P, CH, P])
        self.f_W2 = self.keep("f_W2", [P, CH, P])
        self.f_Wg = self.keep("f_Wg", [P, E])
        self.f_bqk = self.keep("f_bqk", [P, 2])
        self.f_bv = self.keep("f_bv", [P, P])
        self.f_bg = self.keep("f_bg", [E, 1])
        self.f_bh = self.keep("f_bh", [P, CH])
        self.mean = self.keep("mean", [P, TILES])
        self.var = self.keep("var", [P, TILES])
        self.rstd = self.keep("rstd", [P, TILES])
        self.nmr = self.keep("nmr", [P, TILES])
        self.rstd2 = self.keep("rstd2", [P, TILES])
        self.sd = self.keep("sd", [P, TILES])
        self.ve = self.keep("ve", [P, TILES])
        self.w12 = self.keep("w12", [P, E, 2 * F1])
        self.wg = self.keep("wg", [P, 2, E, F1])
        self.w3 = self.keep("w3", [P, 2, E, P])
        self.m_Wg = self.keep("m_Wg", [P, E])
        self.bias3 = self.keep("bias3", [P, E, 3 * F1 + P], BF16)
        self.ones3 = self.keep("ones3", [P, P], BF16)
        self.arena = self.keep("arena", [P, ARENA])
        self.ps = ctx.enter_context(nc.psum_tensor("ps", [P, 8, 512], F32))

    def keep(self, name, shape, dt=F32):
        return self.ctx.enter_context(self.nc.sbuf_tensor(name, shape, dt))

    def const(self, name):
        at, n = CONST_AT[name]
        return self.cst[:, at:at + n]

    def col(self, name):
        n = COLS.index(name)
        return self.cols[:, n:n + 1]

    def row(self, name):
        at, n = ROW_AT[name]
        return self.rows[:, at:at + n]

    def mat(self, name):
        return self.mats[:, MATS.index(name), :]

    def layout(self):
        at = [0]

        def take(*shape, dt=F32):
            n = int(np.prod(shape))
            words = n if dt != BF16 else (n + 1) // 2
            flat = self.arena[:, at[0]:at[0] + words]
            at[0] += words
            assert at[0] <= ARENA, at[0]
            if dt != F32:
                flat = flat.bitcast(dt)
            if len(shape) == 1:
                return flat
            names = "abcdef"[:len(shape)]
            return flat.rearrange(f"p ({' '.join(names)}) -> p {' '.join(names)}",
                                  **{n: s for n, s in zip(names[1:], shape[1:])})
        return take


def semaphores(nc, ctx, prefix, names):
    made = {n: nc.alloc_semaphore(f"{prefix}_{n}") for n in names.split()}
    ctx.callback(nc.all_engine_barrier)
    ctx.callback(nc.clear_and_free_semaphores, list(made.values()))
    return made


def wait_past(eng, sem, count):
    if not (isinstance(count, int) and count <= 0):
        eng.wait_ge(sem, count)


def loop(eng, n, body):
    body(0)
    with eng.Fori(1, n) as i:
        body(i)


def setup(nc, m, dram):
    with ExitStack() as ctx:
        s = semaphores(nc, ctx, "setup", "loaded spread pe split link parts filled rows_ready")
        take = m.layout()
        w1_raw, wg_raw, b1s, wk8, wv8 = take(E, K0), take(E), take(P), take(D), take(D)
        BW = 3 * F1 + P
        bias_raw, bias_rest = take(BW), take(BW)
        bias_parts = take(3, BW, dt=BF16)
        empty = take(ROW)
        LOADS = 18 + len(MATS)
        with nc.Block() as block:
            @block.sync
            def _(sp):
                def load(dst, src):
                    sp.dma_start(dst, src).then_inc(s["loaded"], 16)
                load(m.cst[:, :], dram["consts"])
                load(m.cols[:, :], dram["cols"])
                load(m.rows[:, :], dram["rows"].to_broadcast([P, ROW_COLS]))
                load(m.x[:, :, :], dram["x"].rearrange("(t p) c -> p t c", p=P))
                load(m.f_W2[:, :, :], dram["f_W2"].rearrange("e k d -> (e k) d").rearrange("(c p) d -> p c d", p=P))
                load(m.w12[:, :, 0:F1], dram["m_w1"].rearrange("e p f -> p e f"))
                load(m.w12[:, :, F1:2 * F1], dram["m_w2"].rearrange("e p f -> p e f"))
                for k in range(2):
                    load(m.wg[:, k], dram["m_wg"][:, k * P:(k + 1) * P, :].rearrange("e p f -> p e f"))
                    load(m.w3[:, k], dram["m_w3"][:, k * P:(k + 1) * P, :].rearrange("e p f -> p e f"))
                sp.wait_ge(s["parts"], 3)
                sp.wait_ge(s["rows_ready"], 1)
                for k in range(3):
                    sp.dma_start(m.bias3[k:k + 1, :, :], bias_parts[0:E, k]).then_inc(s["filled"], 16)
                sp.wait_ge(s["rows_ready"], 3)
                for d in dram["slots"]:
                    for q in range(4):
                        n = SLOTS // 4
                        sp.dma_start(d[q * n:(q + 1) * n, :].rearrange("(t p) c -> p t c", p=P),
                                     empty.unsqueeze(1).to_broadcast([P, SLOT_TILES // 4, ROW])).then_inc(s["filled"], 16)
                sp.wait_ge(s["filled"], 16 * 11)
                sp.wait_ge(s["loaded"], 16 * LOADS)

            @block.scalar
            def _(act):
                def load(dst, src):
                    act.dma_start(dst, src).then_inc(s["loaded"], 16)
                load(w1_raw, dram["f_W1"].rearrange("e d k -> d e k"))
                load(wg_raw, dram["f_Wg"])
                load(m.m_Wg[:, :], dram["m_Wg"])
                load(wk8, dram["a_Wk"])
                load(wv8, dram["a_Wv"])
                load(bias_raw[0:E], dram["m_biases"])
                load(b1s[0:1, :], dram["rows"][:, 0:P])
                for n in MATS:
                    load(m.mat(n), dram["f_Wk" if n in ("a_Wk", "a_Wv") else n])

            @block.gpsimd
            def _(pool):
                g = nc.gpsimd
                g.memset(m.ones3[:, :], 1.0)
                g.memset(m.bias3[:, :, :].rearrange("p e n -> p (e n)").bitcast(F32), 0.0).then_inc(s["rows_ready"], 1)
                g.memset(empty[:, 0:P + 1], 0.0).then_inc(s["rows_ready"], 1)
                g.memset(empty.bitcast(I32)[:, P + 1:P + 2], NOWHERE).then_inc(s["rows_ready"], 1)

            @block.tensor
            def _(pe):
                t, ps = nc.tensor, m.ps
                pe.wait_ge(s["loaded"], 16 * LOADS)
                pe.wait_ge(s["link"], 1)
                t.matmul(ps[:, 0, 0:1], m.mat("f_Wq"), m.col("f_b1"), start=True, stop=True)
                t.matmul(ps[:, 0, 1:2], m.mat("f_Wk"), m.col("f_b1"), start=True, stop=True)
                for c in range(CH):
                    t.matmul(ps[:, 0, 2 + c:3 + c], w1_raw[:, 2 * c:2 * c + 2, :].rearrange("p e k -> p (e k)"),
                             m.col("f_b2"), start=True, stop=True)
                t.matmul(ps[0:E, 0, 9:10], wg_raw, m.col("f_b2"), start=True, stop=True)
                t.matmul(ps[:, 1, 0:P], m.mat("a_WqT"), m.const("rope"), start=True, stop=True)
                t.matmul(ps[:, 0, 8:9], m.const("rope"), m.col("a_bq"), start=True, stop=True)
                pe.wait_ge(s["spread"], 1)
                t.matmul(ps[:, 2, 0:P], b1s, m.mat("f_Wv"), start=True, stop=True).then_inc(s["pe"], 1)

            @block.vector
            def _(dve):
                v, ps = nc.vector, m.ps
                v.memset(ps[:, :, :], 0.0).then_inc(s["link"], 1)
                dve.wait_ge(s["loaded"], 16 * LOADS)
                v.tensor_copy(b1s, m.col("f_b1").to_broadcast([P, P])).then_inc(s["spread"], 1)
                v.tensor_copy(m.identb[:, :], m.const("ident"))
                v.tensor_copy(m.maskb[:, 0:4, :], m.const("mask_rows").rearrange("p (a k) -> p a k", a=4))
                v.tensor_copy(m.maskb[:, 4:8, :], m.const("mask_cols").rearrange("p (a k) -> p a k", a=4))
                v.tensor_copy(m.mat("a_Wk").rearrange("p (h d) -> p h d", h=H), wk8.unsqueeze(1).to_broadcast([P, H, D]))
                v.tensor_copy(m.mat("a_Wv").rearrange("p (h d) -> p h d", h=H), wv8.unsqueeze(1).to_broadcast([P, H, D]))
                one = slice(0, E)
                v.tensor_copy(bias_parts[one, 0], bias_raw[one]).then_inc(s["parts"], 1)
                dve.wait_ge(s["parts"], 1)
                v.tensor_tensor(bias_rest[one], bias_raw[one], bias_parts[one, 0], ALU.subtract).then_inc(s["split"], 1)
                dve.wait_ge(s["split"], 1)
                v.tensor_copy(bias_parts[one, 1], bias_rest[one]).then_inc(s["parts"], 1)
                dve.wait_ge(s["parts"], 2)
                v.tensor_tensor(bias_parts[one, 2], bias_rest[one], bias_parts[one, 1], ALU.subtract).then_inc(s["parts"], 1)
                dve.wait_ge(s["pe"], 1)
                v.tensor_copy(m.f_bqk[:, :], ps[:, 0, 0:2])
                v.tensor_copy(m.f_bh[:, :], ps[:, 0, 2:2 + CH])
                v.tensor_copy(m.f_bg[:, :], ps[0:E, 0, 9:10])
                v.tensor_copy(m.col("a_bq"), ps[:, 0, 8:9])
                v.tensor_copy(m.mat("a_WqT"), ps[:, 1, 0:P])
                v.tensor_copy(m.f_bv[:, :], ps[:, 2, 0:P])
                for w in ("f_Wq", "f_Wk", "f_Wv"):
                    v.tensor_scalar(m.mat(w), m.mat(w), m.col("f_g1"), None, ALU.mult)
                v.tensor_scalar(m.f_W1[:, :, :].rearrange("p c k -> p (c k)"), w1_raw.rearrange("p e k -> p (e k)"),
                                m.col("f_g2"), None, ALU.mult)
                v.tensor_scalar(m.f_Wg[:, :], wg_raw, m.col("f_g2"), None, ALU.mult)


def norm_stats(nc, m, name, src, twice=False):
    with ExitStack() as ctx:
        s = semaphores(nc, ctx, name, "stats link sqrt ve")
        take = m.layout()
        take(TILES * P)
        st = take(TILES, 6)
        total, apart, spread_out = take(TILES), take(TILES), take(TILES)
        with nc.Block() as block:
            @block.vector
            def _(dve):
                v, done = nc.vector, [0]

                def link(ins):
                    done[0] += 1
                    ins.then_inc(s["link"], 1)
                    dve.wait_ge(s["link"], done[0])

                with dve.Fori(0, TILES // 4) as i:
                    for u in range(4):
                        v.bn_stats(st[:, i * 4 + u, :], src[:, i * 4 + u, :]).then_inc(s["stats"], 1)
                dve.wait_ge(s["stats"], TILES)
                v.tensor_tensor(total, st[:, :, 1], st[:, :, 4], ALU.add)
                v.tensor_tensor(apart, st[:, :, 1], st[:, :, 4], ALU.subtract)
                link(v.tensor_tensor(spread_out, st[:, :, 2], st[:, :, 5], ALU.add))
                v.tensor_scalar(m.mean[:, :], total, -0.5, None, ALU.mult)
                v.tensor_scalar(m.var[:, :], spread_out, 1.0 / P, None, ALU.mult)
                link(v.scalar_tensor_tensor(out=apart, in0=apart, scalar=0.25, in1=apart, op0=ALU.mult, op1=ALU.mult))
                link(v.tensor_tensor(m.var[:, :], m.var[:, :], apart, ALU.add))
                v.tensor_scalar(m.ve[:, :], m.var[:, :], EPS, None, ALU.add).then_inc(s["ve"], 1)
                dve.wait_ge(s["sqrt"], 1)
                link(v.reciprocal(m.rstd[:, :], m.sd[:, :]))
                v.tensor_tensor(m.nmr[:, :], m.mean[:, :], m.rstd[:, :], ALU.mult)
                if twice:
                    link(v.tensor_tensor(m.ve[:, :], m.var[:, :], m.rstd[:, :], ALU.mult))
                    link(v.tensor_tensor(m.ve[:, :], m.ve[:, :], m.rstd[:, :], ALU.mult))
                    v.tensor_scalar(m.ve[:, :], m.ve[:, :], EPS, None, ALU.add).then_inc(s["ve"], 1)
                    dve.wait_ge(s["sqrt"], 2)
                    v.reciprocal(m.rstd2[:, :], m.sd[:, :])

            @block.scalar
            def _(act):
                for k in range(2 if twice else 1):
                    act.wait_ge(s["ve"], k + 1)
                    nc.scalar.activation(m.sd[:, :], m.ve[:, :], ACT.Sqrt).then_inc(s["sqrt"], 1)


def spread(cols, n):
    return cols[:, bass.ds(n * GT, GT)].unsqueeze(2).to_broadcast([P, GT, P])


def tiles_of(n):
    return bass.ds(n * GT, GT)


def normed(nc, pool, m, s, n, u, src, keep, z):
    g = nc.gpsimd
    out = z[:, u] if keep is None else keep[:, tiles_of(n), :]
    if keep is None:
        wait_past(pool, s["zt_ps"], n - 1)
    g.tensor_tensor(out, src[:, tiles_of(n), :], spread(m.rstd, n), ALU.mult).then_inc(s["scaled"], 1)
    pool.wait_ge(s["scaled"], n + 1)
    g.tensor_tensor(out, out, spread(m.nmr, n), ALU.add).then_inc(s["z" if keep is None else "shifted"], 1)
    if keep is not None:
        pool.wait_ge(s["shifted"], n + 1)
        wait_past(pool, s["zt_ps"], n - 1)
        g.tensor_tensor(z[:, u], out, spread(m.rstd2, n), ALU.mult).then_inc(s["z"], 1)


def attention_operands(nc, m, name, weights, biases, v_bias, dram, twice):
    Wq, Wk, Wv = weights
    with ExitStack() as ctx:
        s = semaphores(nc, ctx, name, "scaled shifted z zt_ps zt q_ps k_ps v_ps top rest mid low v stored0 stored1")
        take = m.layout()
        val = take(TILES, H, D + 1)
        z = take(2, GT, P)
        zt = take(2, GN)
        parts = take(2, 2, 3, GN, dt=BF16)
        rest = take(2, 2, GN)
        psT = [m.ps[:, u, :] for u in range(2)]
        psQK = [[m.ps[:, 2 + 2 * u + w, :] for w in range(2)] for u in range(2)]
        psV = [m.ps[:, 6 + u, :] for u in range(2)]
        with nc.Block() as block:
            @block.gpsimd
            def _(pool):
                g = nc.gpsimd
                g.memset(val[:, :, :, D], 1.0)

                def body(i):
                    for u in range(2):
                        n = i * 2 + u
                        normed(nc, pool, m, s, n, u, m.x, m.xi if twice else None, z)
                        if not twice:
                            g.tensor_tensor(m.x[:, tiles_of(n), :], m.x[:, tiles_of(n), :],
                                            m.row("a_bo").unsqueeze(1).to_broadcast([P, GT, P]), ALU.add)
                loop(pool, GROUPS // 2, body)

            @block.tensor
            def _(pe):
                t = nc.tensor

                def body(i):
                    for u in range(2):
                        n = i * 2 + u
                        pe.wait_ge(s["z"], n + 1)
                        wait_past(pe, s["zt"], n - 1)
                        for k in range(GT):
                            last = t.transpose(psT[u][:, k * P:(k + 1) * P], z[:, u, k, :], m.const("ident"))
                        last.then_inc(s["zt_ps"], 1)
                        pe.wait_ge(s["zt"], n + 1)
                        wait_past(pe, s["rest"], 2 * n - 3)
                        t.matmul(psQK[u][0], Wq, zt[:, u], start=True, stop=True).then_inc(s["q_ps"], 1)
                        wait_past(pe, s["rest"], 2 * n - 2)
                        t.matmul(psQK[u][1], Wk, zt[:, u], start=True, stop=True).then_inc(s["k_ps"], 1)
                        wait_past(pe, s["v"], n - 1)
                        for k in range(GT):
                            last = t.matmul(psV[u][:, k * P:(k + 1) * P], zt[:, u, k * P:(k + 1) * P], Wv,
                                            start=True, stop=True)
                        last.then_inc(s["v_ps"], 1)
                loop(pe, GROUPS // 2, body)

            @block.scalar
            def _(act):
                a = nc.scalar

                def body(i):
                    for u in range(2):
                        n = i * 2 + u
                        act.wait_ge(s["zt_ps"], n + 1)
                        wait_past(act, s["v_ps"], n - 1)
                        a.activation(zt[:, u], psT[u], ACT.Copy).then_inc(s["zt"], 1)
                        wait_past(act, s[f"stored{u}"], i * (16 * 9))
                        for w, ready in enumerate(("q_ps", "k_ps")):
                            act.wait_ge(s[ready], n + 1)
                            a.activation(parts[:, u, w, 0], psQK[u][w], ACT.Identity, bias=biases[w])\
                                .then_inc(s["top"], 1)
                loop(act, GROUPS // 2, body)

            @block.vector
            def _(dve):
                v = nc.vector

                def body(i):
                    for u in range(2):
                        n = i * 2 + u
                        for w in range(2):
                            dve.wait_ge(s["top"], 2 * n + w + 1)
                            v.scalar_tensor_tensor(out=rest[:, u, w], in0=psQK[u][w], scalar=biases[w],
                                                   in1=parts[:, u, w, 0], op0=ALU.add, op1=ALU.subtract)\
                                .then_inc(s["rest"], 1)
                            dve.wait_ge(s["rest"], 2 * n + w + 1)
                            v.tensor_copy(parts[:, u, w, 1], rest[:, u, w]).then_inc(s["mid"], 1)
                        dve.wait_ge(s["v_ps"], n + 1)
                        for k in range(GT):
                            last = v.tensor_tensor(val[:, n * GT + k, :, 0:D],
                                                   psV[u][:, k * P:(k + 1) * P].rearrange("p (h d) -> p h d", h=H),
                                                   v_bias.rearrange("p (h d) -> p h d", h=H), ALU.add)
                        last.then_inc(s["v"], 1)
                        for w in range(2):
                            dve.wait_ge(s["mid"], 2 * n + w + 1)
                            v.tensor_tensor(parts[:, u, w, 2], rest[:, u, w], parts[:, u, w, 1], ALU.subtract)\
                                .then_inc(s["low"], 1)
                loop(dve, GROUPS // 2, body)

            @block.sync
            def _(sp):
                def store(i):
                    for u in range(2):
                        n = i * 2 + u
                        tok = bass.ds(n * GN, GN)
                        sp.wait_ge(s["low"], 2 * n + 2)
                        for k in range(3):
                            sp.dma_start(dram["q_parts"][:, k, :, tok], parts[:, u, 0, k]).then_inc(s[f"stored{u}"], 16)
                        for r, k in enumerate(PART_K):
                            sp.dma_start(dram["k_parts"][:, r, :, tok], parts[:, u, 1, k]).then_inc(s[f"stored{u}"], 16)
                loop(sp, GROUPS // 2, store)
                for u in range(2):
                    sp.wait_ge(s[f"stored{u}"], GROUPS // 2 * (16 * 9))


def attention(nc, m, name, Wo, dram, causal, out):
    LOADS, SHIFTS = 4, 2
    with ExitStack() as ctx:
        s = semaphores(nc, ctx, name, "zeroed loaded0 loaded1 loaded2 loaded3 row_scores maxed mx_t shift_hi shift_lo "
                       "shifted0 shifted1 col_scores probs vals pv pv_sb ot_ps recip otok otok_t ot proj added")
        loaded = [s[f"loaded{c}"] for c in range(QUADS)]
        shifted = [s[f"shifted{c}"] for c in range(2)]
        take = m.layout()
        val = take(TILES, H, D + 1)
        qr = take(QUADS, QH, T, dt=BF16)
        kr = take(QUADS, QH, T, dt=BF16)
        vals = take(QUADS, 2, QH, D + 1)
        probs = take(2, QH, 2, T)
        mx = take(2, 2, QH)
        shift = take(2, 2, T, dt=BF16)
        pv_sb = take(2, T)
        rec = take(2, QH)
        otok = take(2, H, D)
        ot = take(T)
        S1 = [m.ps[:, u, :] for u in range(2)]
        S2 = [m.ps[:, 2 + u, :] for u in range(2)]
        PV, FIN, OT = m.ps[:, 4, 0:T], m.ps[:, 5, 0:T], m.ps[:, 6, 0:T]
        MX = m.ps[0:QH, 7, 0:T]
        maskr = m.maskb[:, 0:4, :].rearrange("p (q a) k -> p q (a k)", q=2)
        maskc = m.maskb[:, 4:8, :].rearrange("p (q a) k -> p q (a k)", q=2)

        def at(b, c, ahead):
            b2, c2 = b + (c + ahead) // QUADS, (c + ahead) % QUADS
            return b2, c2, b2 * QUADS + c2

        def quads(eng, slot):
            for c in range(QUADS):
                slot(0, c, True, False)
            with eng.Fori(1, B - 1) as b:
                for c in range(QUADS):
                    slot(b, c, False, False)
            for c in range(QUADS):
                slot(B - 1, c, False, True)

        with nc.Block() as block:
            @block.gpsimd
            def _(pool):
                g = nc.gpsimd
                g.memset(qr, 0.0)
                g.memset(kr, 0.0).then_inc(s["zeroed"], 1)
                pool.wait_ge(s["zeroed"], 1)
                g.memset(kr[SHIFT_ROW:P], -1.0).then_inc(s["zeroed"], 1)
                pool.wait_ge(s["zeroed"], 2)

                def slot(b, c, first, last):
                    n = b * QUADS + c
                    wait_past(pool, s["pv"], n - 3)
                    g.tensor_copy(vals[:, c], val[:, bass.ds(b * 2, 2), QH * c:QH * c + QH, :]).then_inc(s["vals"], 1)
                quads(pool, slot)

            @block.sync
            def _(sp):
                def load(b, c):
                    tok, heads = bass.ds(b * T, T), slice(QH * c, QH * c + QH)
                    at_row = 0
                    for count in (3, 2, 1):
                        sp.dma_start(qr[at_row:at_row + D * count, c],
                                     dram["q_parts"][heads, 0:count, :, tok].rearrange("h a d t -> (a d) h t"))\
                            .then_inc(loaded[c], 16)
                        at_row += D * count
                    sp.dma_start(kr[0:SPLIT_ROWS, c],
                                 dram["k_parts"][heads, :, :, tok].rearrange("h a d t -> (a d) h t"))\
                        .then_inc(loaded[c], 16)

                def store_shift(b, c):
                    sp.wait_ge(s["shift_lo"], b * QUADS + c + 1)
                    for k in range(2):
                        sp.dma_start(qr[SHIFT_ROW + k:SHIFT_ROW + k + 1, c], shift[0:QH, c % 2, k])\
                            .then_inc(shifted[c % 2], 16)

                def slot(b, c, first, last):
                    n = b * QUADS + c
                    if not last:
                        sp.wait_ge(s["col_scores"], QH * n + QH)
                        load(b + 1, c)
                    if not (last and c >= 2):
                        store_shift(*at(b, c, 2)[:2])

                sp.wait_ge(s["zeroed"], 2)
                for c in range(QUADS):
                    load(0, c)
                store_shift(0, 0)
                store_shift(0, 1)
                quads(sp, slot)

            @block.tensor
            def _(pe):
                t = nc.tensor

                def row_scores(b, c, n, j):
                    if j == 0:
                        pe.wait_ge(loaded[c], (b + 1) * (16 * LOADS))
                    wait_past(pe, s["maxed"], n * QH + j - 1)
                    for qt in range(2):
                        o = S1[j % 2][:, qt * T:(qt + 1) * T]
                        last = t.matmul(o, qr[0:SHIFT_ROW, c, j, qt * P:(qt + 1) * P], kr[0:SHIFT_ROW, c, j],
                                        start=True, stop=not causal)
                        if causal:
                            last = t.matmul(o, m.identb[:, :], maskr[:, qt], start=False, stop=True)
                    last.then_inc(s["row_scores"], 1)

                def col_scores(b, c, n, j):
                    if j == 0:
                        pe.wait_ge(shifted[c % 2], (b * 2 + c // 2 + 1) * (16 * SHIFTS))
                    wait_past(pe, s["probs"], n * QH + j - 1)
                    for kt in range(2):
                        o = S2[j % 2][:, kt * T:(kt + 1) * T]
                        last = t.matmul(o, kr[0:SHIFT_ROW + 2, c, j, kt * P:(kt + 1) * P],
                                        qr[0:SHIFT_ROW + 2, c, j], start=True, stop=not causal)
                        if causal:
                            last = t.matmul(o, m.identb[:, :], maskc[:, kt], start=False, stop=True)
                    last.then_inc(s["col_scores"], 1)

                def turn_max(b, c, n):
                    pe.wait_ge(s["maxed"], n * QH + QH)
                    wait_past(pe, s["shift_lo"], n)
                    for qt in range(2):
                        last = t.transpose(MX[:, qt * P:(qt + 1) * P], mx[:, c % 2, qt], m.const("ident"))
                    last.then_inc(s["mx_t"], 1)

                def values(b, c, n):
                    pe.wait_ge(s["probs"], QH * n + QH)
                    pe.wait_ge(s["vals"], n + 1)
                    wait_past(pe, s["pv_sb"], n)
                    for kt in range(2):
                        for j in range(QH):
                            last = t.matmul(PV[32 * j:32 * j + D + 1, :], vals[:, c, kt, j, :], probs[:, c % 2, j, kt],
                                            start=(kt == 0), stop=(kt == 1))
                    last.then_inc(s["pv"], 1)

                def turn_heads(b, c, n):
                    pe.wait_ge(s["pv_sb"], n + 1)
                    wait_past(pe, s["otok"], n)
                    for qt in range(2):
                        last = t.transpose(OT[:, qt * P:(qt + 1) * P], pv_sb[:, c % 2, qt * P:(qt + 1) * P],
                                           m.const("ident"))
                    last.then_inc(s["ot_ps"], 1)

                def turn_all(b):
                    pe.wait_ge(s["otok"], (b + 1) * QUADS)
                    wait_past(pe, s["added"], b)
                    for qt in range(2):
                        last = t.transpose(FIN[:, qt * P:(qt + 1) * P], otok[:, qt].rearrange("p h d -> p (h d)"),
                                           m.const("ident"))
                    last.then_inc(s["otok_t"], 1)

                def project(b):
                    pe.wait_ge(s["ot"], b + 1)
                    for qt in range(2):
                        last = t.matmul(FIN[:, qt * P:(qt + 1) * P], ot[:, qt * P:(qt + 1) * P], Wo, start=True, stop=True)
                    last.then_inc(s["proj"], 1)

                def slot(b, c, first, last):
                    for j in range(QH):
                        if not (last and c >= 2):
                            row_scores(*at(b, c, 2), j)
                        col_scores(*at(b, c, 0), j)
                    if not (first and c < 1):
                        values(*at(b, c, -1))
                    if not (first and c < 2):
                        turn_heads(*at(b, c, -2))
                    if not first and c == 2:
                        turn_all(b - 1)
                    if not first and c == 3:
                        project(b - 1)
                    if not (last and c >= 2):
                        turn_max(*at(b, c, 2))

                for c in range(2):
                    for j in range(QH):
                        row_scores(0, c, c, j)
                    turn_max(0, c, c)
                quads(pe, slot)
                values(*at(B - 1, 3, 0))
                turn_heads(*at(B - 1, 2, 0))
                turn_heads(*at(B - 1, 3, 0))
                turn_all(B - 1)
                project(B - 1)

            @block.scalar
            def _(act):
                a = nc.scalar

                def exponentials(b, c, n):
                    wait_past(act, s["pv"], n - 1)
                    for j in range(QH):
                        act.wait_ge(s["col_scores"], n * QH + j + 1)
                        a.activation(probs[:, c % 2, j].rearrange("p t q -> p (t q)"), S2[j % 2], ACT.Exp, scale=SCALE)\
                            .then_inc(s["probs"], 1)

                def copy_values(b, c, n):
                    act.wait_ge(s["pv"], n + 1)
                    wait_past(act, s["ot_ps"], n - 1)
                    a.activation(pv_sb[:, c % 2], PV, ACT.Copy).then_inc(s["pv_sb"], 1)

                def copy_heads(b):
                    act.wait_ge(s["otok_t"], b + 1)
                    a.activation(ot, FIN, ACT.Copy).then_inc(s["ot"], 1)

                def shift_high(b, c, n):
                    act.wait_ge(s["mx_t"], n + 1)
                    wait_past(act, shifted[c % 2], (b * 2 + c // 2) * (16 * SHIFTS))
                    a.activation(shift[0:QH, c % 2, 0], MX, ACT.Copy).then_inc(s["shift_hi"], 1)

                def slot(b, c, first, last):
                    exponentials(b, c, b * QUADS + c)
                    if not (first and c < 1):
                        copy_values(*at(b, c, -1))
                    if not first and c == 2:
                        copy_heads(b - 1)
                    if not (last and c >= 2):
                        shift_high(*at(b, c, 2))

                shift_high(0, 0, 0)
                shift_high(0, 1, 1)
                quads(act, slot)
                copy_values(*at(B - 1, 3, 0))
                copy_heads(B - 1)

            @block.vector
            def _(dve):
                v = nc.vector

                def maxima(b, c, n):
                    wait_past(dve, s["mx_t"], n - 1)
                    for j in range(QH):
                        dve.wait_ge(s["row_scores"], n * QH + j + 1)
                        v.tensor_reduce(mx[:, c % 2, :, j], S1[j % 2].rearrange("p (q k) -> p q k", q=2),
                                        AX.X, ALU.max).then_inc(s["maxed"], 1)

                def shift_low(b, c, n):
                    dve.wait_ge(s["shift_hi"], n + 1)
                    v.tensor_tensor(shift[0:QH, c % 2, 1], MX, shift[0:QH, c % 2, 0], ALU.subtract)\
                        .then_inc(s["shift_lo"], 1)

                def normalise(b, c, n):
                    dve.wait_ge(s["ot_ps"], n + 1)
                    o = OT.rearrange("p (q j r) -> p q j r", q=2, j=QH)
                    wait_past(dve, s["otok"], n)
                    v.reciprocal(rec, o[:, :, :, D]).then_inc(s["recip"], 1)
                    dve.wait_ge(s["recip"], n + 1)
                    if c == 0:
                        wait_past(dve, s["otok_t"], b)
                    v.tensor_tensor(otok[:, :, QH * c:QH * c + QH, :], o[:, :, :, 0:D],
                                    rec.unsqueeze(3).to_broadcast([P, 2, QH, D]), ALU.mult).then_inc(s["otok"], 1)

                def add(b):
                    dve.wait_ge(s["proj"], b + 1)
                    o = out[:, bass.ds(b * 2, 2), :]
                    v.tensor_tensor(o, FIN.rearrange("p (t c) -> p t c", t=2), o, ALU.add).then_inc(s["added"], 1)

                def slot(b, c, first, last):
                    if not (last and c >= 2):
                        maxima(*at(b, c, 2))
                    if not (first and c < 2):
                        normalise(*at(b, c, -2))
                    if not first and c == 3:
                        add(b - 1)
                    if not (last and c >= 2):
                        shift_low(*at(b, c, 2))

                for c in range(2):
                    maxima(0, c, c)
                    shift_low(0, c, c)
                quads(dve, slot)
                normalise(*at(B - 1, 2, 0))
                normalise(*at(B - 1, 3, 0))
                add(B - 1)


def turned(nc, pe, m, s, n, u, z, psT):
    pe.wait_ge(s["z"], n + 1)
    wait_past(pe, s["zt"], n - 1)
    for k in range(GT):
        last = nc.tensor.transpose(psT[u][:, k * P:(k + 1) * P], z[:, u, k, :], m.const("ident"))
    last.then_inc(s["zt_ps"], 1)


class Routing:

    def __init__(self, m):
        at = [ARENA]

        def take(*shape):
            n = int(np.prod(shape))
            at[0] -= n
            flat = m.arena[:, at[0]:at[0] + n]
            return flat if len(shape) == 1 else flat.rearrange("p (t e) -> p t e", e=shape[1])
        self.logits = take(TILES, E)
        self.one = [take(TILES, E) for _ in range(2)]
        self.prob = [take(TILES) for _ in range(2)]
        self.top = [take(TILES) for _ in range(2)]
        self.weights = take(TILES, E)
        self.place = [take(TILES) for _ in range(2)]
        self.expert = take(SLOT_TILES)


def gate(nc, m, name, r, src, Wg, bias, z_keep, zt_keep):
    with ExitStack() as ctx:
        s = semaphores(nc, ctx, name, "scaled shifted z zt_ps zt kept logit_ps logit_sb turned logits")
        take = m.layout()
        if zt_keep:
            take(TILES, P)
        else:
            take(TILES, 2, ROW)
        z = take(2, GT, P)
        zt = take(2, GN)
        lt = take(2, GN)
        psT = [m.ps[:, u, :] for u in range(2)]
        psL = [m.ps[0:E, 2 + u, :] for u in range(2)]
        psR = [m.ps[:, 4 + u, 0:GT * E] for u in range(2)]
        with nc.Block() as block:
            @block.gpsimd
            def _(pool):
                def body(i):
                    for u in range(2):
                        n = i * 2 + u
                        if z_keep is not None:
                            wait_past(pool, s["kept"], n - 1)
                        normed(nc, pool, m, s, n, u, src, None, z)
                loop(pool, GROUPS // 2, body)

            @block.tensor
            def _(pe):
                t = nc.tensor

                def turn_back(n, u):
                    pe.wait_ge(s["logit_sb"], n + 1)
                    wait_past(pe, s["logits"], n - 1)
                    for k in range(GT):
                        last = t.matmul(psR[u][:, k * E:(k + 1) * E], lt[0:E, u, k * P:(k + 1) * P],
                                        m.const("ident")[0:E, 0:E], start=True, stop=True)
                    last.then_inc(s["turned"], 1)

                def body(i):
                    for u in range(2):
                        n = i * 2 + u
                        turned(nc, pe, m, s, n, u, z, psT)
                        pe.wait_ge(s["zt"], n + 1)
                        wait_past(pe, s["logit_sb"], n - 1)
                        t.matmul(psL[u], Wg, zt[:, u], start=True, stop=True).then_inc(s["logit_ps"], 1)
                        turn_back(n, u)
                loop(pe, GROUPS // 2, body)

            @block.scalar
            def _(act):
                a = nc.scalar

                def body(i):
                    for u in range(2):
                        n = i * 2 + u
                        act.wait_ge(s["zt_ps"], n + 1)
                        wait_past(act, s["logit_ps"], n - 1)
                        if zt_keep:
                            wait_past(act, s["kept"], n - 1)
                        a.activation(zt[:, u], psT[u], ACT.Copy).then_inc(s["zt"], 1)
                        act.wait_ge(s["logit_ps"], n + 1)
                        wait_past(act, s["turned"], n - 1)
                        a.activation(lt[0:E, u], psL[u], ACT.Identity, bias=bias).then_inc(s["logit_sb"], 1)
                loop(act, GROUPS // 2, body)

            @block.vector
            def _(dve):
                v = nc.vector

                def body(i):
                    for u in range(2):
                        n = i * 2 + u
                        if zt_keep:
                            dve.wait_ge(s["zt"], n + 1)
                            v.tensor_copy(m.arena[:, bass.ds(n * GN, GN)], zt[:, u]).then_inc(s["kept"], 1)
                        else:
                            dve.wait_ge(s["z"], n + 1)
                            for k in range(2):
                                last = v.tensor_copy(z_keep[:, tiles_of(n), k, 0:P], z[:, u])
                            last.then_inc(s["kept"], 1)
                        dve.wait_ge(s["turned"], n + 1)
                        v.tensor_copy(r.logits[:, tiles_of(n), :], psR[u].rearrange("p (t e) -> p t e", e=E))\
                            .then_inc(s["logits"], 1)
                loop(dve, GROUPS // 2, body)


def choose(nc, m, name, r, dispatch=None):
    with ExitStack() as ctx:
        s = semaphores(nc, ctx, name, "link gap exp chosen ranks counts")
        take = m.layout()
        take(TILES, 2, ROW)
        best, key, key_top, masked = take(TILES, E), take(TILES, E), take(TILES), take(TILES, E)
        gap, e_gap = take(TILES), take(TILES)
        ones, both = take(P), take(TILES, E)
        total, keep, upto = take(E, TILES), take(E, TILES), take(E, TILES)
        pos, count, tiles, ends, bases, one8 = take(TILES, E), take(E), take(E), take(E), take(E), take(E)
        whole = take(E).bitcast(I32)
        over, fexp, fpl = take(SLOT_TILES, E), take(SLOT_TILES), take(TILES)
        RANK, TOTAL = m.ps[:, 0, 0:TILES * E], m.ps[:, 1, 0:TILES * E]

        def along(x, n=E):
            return x.unsqueeze(2).to_broadcast([P, TILES, n])

        with nc.Block() as block:
            @block.vector
            def _(dve):
                v, done = nc.vector, [0]

                def link(ins):
                    done[0] += 1
                    ins.then_inc(s["link"], 1)
                    dve.wait_ge(s["link"], done[0])

                rev = m.const("rev").unsqueeze(1).to_broadcast([P, TILES, E])
                left = r.logits
                for c in range(2):
                    link(v.tensor_reduce(r.top[c], left, AX.X, ALU.max))
                    link(v.tensor_tensor(best, left, along(r.top[c]), ALU.is_equal))
                    link(v.tensor_tensor(key, best, rev, ALU.mult))
                    link(v.tensor_reduce(key_top, key, AX.X, ALU.max))
                    link(v.tensor_tensor(r.one[c], rev, along(key_top), ALU.is_equal))
                    if c == 0:
                        link(v.scalar_tensor_tensor(out=masked, in0=r.one[0], scalar=-3e38, in1=r.logits,
                                                    op0=ALU.mult, op1=ALU.add))
                        left = masked
                v.tensor_tensor(gap, r.top[1], r.top[0], ALU.subtract).then_inc(s["gap"], 1)
                if dispatch is not None:
                    v.memset(ones, 1.0)
                    v.tensor_tensor(both, r.one[0], r.one[1], ALU.add).then_inc(s["chosen"], 1)
                    v.memset(one8, 1.0)
                    link(v.memset(keep, 1.0))
                    link(v.memset(keep[:, :, 0:1], 0.0))
                dve.wait_ge(s["exp"], 1)
                link(v.tensor_scalar(gap, e_gap, 1.0, None, ALU.add))
                link(v.reciprocal(r.prob[0], gap))
                link(v.tensor_tensor(r.prob[1], r.prob[0], e_gap, ALU.mult))
                if dispatch is None:
                    link(v.tensor_tensor(best, r.one[0], along(r.prob[0]), ALU.mult))
                    link(v.tensor_tensor(key, r.one[1], along(r.prob[1]), ALU.mult))
                    link(v.tensor_tensor(r.weights, best, key, ALU.add))
                    return
                dve.wait_ge(s["counts"], 1)
                link(v.tensor_copy(total, TOTAL.rearrange("p (t e) -> p e t", e=E)))
                link(v.tensor_tensor_scan(upto.rearrange("p e t -> p (e t)"), keep.rearrange("p e t -> p (e t)"),
                                          total.rearrange("p e t -> p (e t)"), 0.0, ALU.mult, ALU.add))
                link(v.tensor_scalar(count, upto[:, :, TILES - 1], float(P - 1), None, ALU.add))
                link(v.tensor_copy(whole, count))
                link(v.tensor_scalar(whole, whole, 7, None, ALU.arith_shift_right))
                link(v.tensor_copy(tiles, whole))
                link(v.tensor_tensor_scan(ends, one8, tiles, 0.0, ALU.mult, ALU.add))
                link(v.tensor_tensor(bases, ends, tiles, ALU.subtract))
                link(v.tensor_scalar(bases, bases, float(P), None, ALU.mult))
                link(v.tensor_tensor(upto, upto, total, ALU.subtract))
                link(v.tensor_tensor(upto, upto, bases.unsqueeze(2).to_broadcast([P, E, TILES]), ALU.add))
                link(v.tensor_tensor(pos, RANK.rearrange("p (t e) -> p t e", e=E), upto.rearrange("p e t -> p t e"), ALU.add))
                for c in range(2):
                    link(v.tensor_tensor(key, r.one[c], pos, ALU.mult))
                    link(v.tensor_reduce(fpl, key, AX.X, ALU.add))
                    link(v.tensor_copy(r.place[c].bitcast(I32), fpl))
                    v.tensor_scalar(dispatch[:, :, c, P], r.prob[c], 0.5, None, ALU.mult)
                    link(v.tensor_scalar(fpl, m.const("token"), float(c * TOKENS), None, ALU.add))
                    link(v.tensor_copy(dispatch.bitcast(I32)[:, :, c, P + 1], fpl))
                link(v.tensor_tensor(over, m.const("slot").unsqueeze(2).to_broadcast([P, SLOT_TILES, E]),
                                     ends.unsqueeze(1).to_broadcast([P, SLOT_TILES, E]), ALU.is_ge))
                link(v.tensor_reduce(fexp, over, AX.X, ALU.add))
                link(v.tensor_scalar(fexp, fexp, float(E - 1), None, ALU.min))
                link(v.tensor_copy(r.expert.bitcast(I32), fexp))

            @block.scalar
            def _(act):
                act.wait_ge(s["gap"], 1)
                nc.scalar.activation(e_gap, gap, ACT.Exp).then_inc(s["exp"], 1)

            if dispatch is not None:
                @block.tensor
                def _(pe):
                    t = nc.tensor
                    pe.wait_ge(s["chosen"], 1)
                    flat = both.rearrange("p t e -> p (t e)")
                    t.matmul(RANK, m.const("before"), flat, start=True, stop=True)
                    t.matmul(TOTAL, ones, flat, start=True, stop=True).then_inc(s["counts"], 1)


def experts_dense(nc, m, name, r):
    with ExitStack() as ctx:
        s = semaphores(nc, ctx, name, "w w_ps wt wide hidden relu scaled y base link done")
        take = m.layout()
        zt_all = take(TILES * P)
        w = take(2, GT, E)
        wt = take(2, GN)
        hid = take(2, GN)
        hs = take(2, CH, GN)
        psC = m.ps[0:E, 0, :]
        psB = [m.ps[:, 1 + u, :] for u in range(2)]
        psH = [m.ps[:, 3 + u, :] for u in range(2)]
        psY = [m.ps[:, 5 + u, :] for u in range(2)]
        with nc.Block() as block:
            @block.gpsimd
            def _(pool):
                def body(i):
                    for u in range(2):
                        n = i * 2 + u
                        wait_past(pool, s["w_ps"], n - 1)
                        nc.gpsimd.tensor_copy(w[:, u], r.weights[:, tiles_of(n), :]).then_inc(s["w"], 1)
                loop(pool, GROUPS // 2, body)

            @block.tensor
            def _(pe):
                t = nc.tensor

                def products(n, u):
                    pe.wait_ge(s["scaled"], n * CH + CH)
                    wait_past(pe, s["done"], n - 1)
                    for k in range(GT):
                        for c in range(CH):
                            last = t.matmul(psY[u][:, k * P:(k + 1) * P], hs[:, u, c, k * P:(k + 1) * P],
                                            m.f_W2[:, c, :], start=(c == 0), stop=(c == CH - 1))
                    last.then_inc(s["y"], 1)

                def body(i):
                    for u in range(2):
                        n = i * 2 + u
                        pe.wait_ge(s["w"], n + 1)
                        wait_past(pe, s["wt"], n)
                        for k in range(GT):
                            last = t.transpose(psC[:, k * P:(k + 1) * P], w[:, u, k, :], m.const("ident"))
                        last.then_inc(s["w_ps"], 1)
                        for c in range(CH):
                            wait_past(pe, s["relu"], n * CH + c - 1)
                            t.matmul(psH[c % 2], m.f_W1[:, c, :], zt_all[:, bass.ds(n * GN, GN)],
                                     start=True, stop=True).then_inc(s["hidden"], 1)
                            if c == 0:
                                pe.wait_ge(s["wt"], n + 1)
                            wait_past(pe, s["scaled"], n * CH + c - 1)
                            t.matmul(psB[c % 2], m.const("sel")[0:E, c * P:(c + 1) * P], wt[0:E, u],
                                     start=True, stop=True).then_inc(s["wide"], 1)
                            if c == 1 and not (isinstance(n, int) and n == 0):
                                products(n - 1, 1 - u)
                loop(pe, GROUPS // 2, body)
                products(GROUPS - 1, 1)

            @block.scalar
            def _(act):
                a = nc.scalar

                def body(i):
                    for u in range(2):
                        n = i * 2 + u
                        act.wait_ge(s["w_ps"], n + 1)
                        wait_past(act, s["wide"], (n - 1) * CH)
                        a.activation(wt[0:E, u], psC, ACT.Copy).then_inc(s["wt"], 1)
                        for c in range(CH):
                            act.wait_ge(s["hidden"], n * CH + c + 1)
                            wait_past(act, s["scaled"], n * CH + c - 1)
                            a.activation(hid[:, c % 2], psH[c % 2], ACT.Relu, bias=m.f_bh[:, c:c + 1]).then_inc(s["relu"], 1)
                loop(act, GROUPS // 2, body)

            @block.vector
            def _(dve):
                v = nc.vector

                def finish(n, u):
                    xs = m.x[:, tiles_of(n), :]
                    v.scalar_tensor_tensor(out=xs, in0=m.xi[:, tiles_of(n), :], scalar=0.5, in1=xs,
                                           op0=ALU.mult, op1=ALU.add).then_inc(s["base"], 1)
                    dve.wait_ge(s["y"], n + 1)
                    dve.wait_ge(s["base"], n + 1)
                    v.scalar_tensor_tensor(out=xs, in0=psY[u].rearrange("p (t c) -> p t c", t=GT), scalar=0.5, in1=xs,
                                           op0=ALU.mult, op1=ALU.add).then_inc(s["done"], 1)

                def body(i):
                    for u in range(2):
                        n = i * 2 + u
                        for c in range(CH):
                            dve.wait_ge(s["relu"], n * CH + c + 1)
                            dve.wait_ge(s["wide"], n * CH + c + 1)
                            if c == 0:
                                wait_past(dve, s["y"], n - 1)
                            v.tensor_tensor(hs[:, u, c], hid[:, c % 2], psB[c % 2], ALU.mult).then_inc(s["scaled"], 1)
                            if c == 2 and not (isinstance(n, int) and n == 0):
                                finish(n - 1, 1 - u)
                loop(dve, GROUPS // 2, body)
                finish(GROUPS - 1, 1)


def scatter(nc, m, name, r, rows, slots):
    with ExitStack() as ctx:
        s = semaphores(nc, ctx, name, "sent")
        with nc.Block() as block:
            @block.gpsimd
            def _(pool):
                for t in range(TILES):
                    for c in range(2):
                        pool.indirect_dma_start(
                            slots, bass.IndirectOffsetOnAxis(ap=r.place[c].bitcast(I32)[:, t:t + 1], axis=0),
                            rows[:, t, c, :], None).then_inc(s["sent"], 16)
                pool.wait_ge(s["sent"], 2 * TILES * 16)


def experts_routed(nc, m, name, r, slots, results):
    with ExitStack() as ctx:
        s = semaphores(nc, ctx, name, "load0 load1 load2 load3 load4 load5 load6 load7 zt_ps zt up x1 gated gated_t gated_sb mix act act_t act_sb down out "
                       "sent0 sent1 taken")
        take = m.layout()
        rows = take(RING, ROW)
        zt, x1, gated, gated_t = take(2, P), take(2, F1), take(2, F1), take(2, F1)
        acts, acts_t, out = take(2, F1), take(2, F1), take(2, P)
        psZ, psU = m.ps[:, 0, 0:P], m.ps[:, 1, :]
        psG, psM = m.ps[:, 2, 0:F1], m.ps[:, 3, 0:F1]
        psA, psD = m.ps[:, 4, 0:F1], m.ps[:, 5, 0:P]

        def each(eng, parts, reach):
            n = SLOT_TILES // RING
            for u in range(RING):
                parts(u, u, lambda d, t=u: t - d >= 0)
            with eng.Fori(1, n) as i:
                for u in range(RING):
                    parts(i * RING + u, u, lambda d: True)
            for t in range(SLOT_TILES, SLOT_TILES + reach):
                parts(t, t % RING, lambda d, t=t: t - d < SLOT_TILES)

        def sent_count(t, u, back):
            if isinstance(t, int):
                return (t - back) // 2 * 16 + 16 if t >= back else 0
            return (t - u) * 8 + (u // 2 - back // 2 + 1) * 16

        with nc.Block() as block:
            @block.sync
            def _(sp):
                def parts(t, u, live):
                    if live(0):
                        wait_past(sp, s[f"sent{u % 2}"], sent_count(t, u, RING))
                        sp.dma_start(rows[:, u], slots[bass.ds(t * P, P), :]).then_inc(s[f"load{u}"], 16)
                each(sp, parts, 0)

            @block.tensor
            def _(pe):
                tn = nc.tensor
                ident = m.const("ident")

                def turn(ps, src, n):
                    for k in range(n):
                        last = tn.transpose(ps[:, k * P:(k + 1) * P], src[:, k * P:(k + 1) * P], ident)
                    return last

                held = [tn.alloc_register(f"{name}_expert{u}") for u in range(RING)]

                def fetch_expert(t, u):
                    tn.reg_load(held[u], r.expert.bitcast(I32)[0:1, bass.ds(t, 1)])

                def product(ps, lhs, e, weights, bias_at, bias_n, sem):
                    for k, w in enumerate(weights):
                        tn.matmul(ps, lhs[:, k * P:(k + 1) * P], w[:, bass.ds(e, 1), :].rearrange("p o f -> p (o f)"),
                                  start=(k == 0), stop=False)
                    tn.matmul(ps, m.ones3[:, :],
                              m.bias3[:, bass.ds(e, 1), bias_at:bias_at + bias_n].rearrange("p o f -> p (o f)"),
                              start=False, stop=True).then_inc(sem, 1)

                def turn_rows(t, u):
                    pe.wait_ge(s[f"load{u}"], (t - u) * 2 + 16)
                    wait_past(pe, s["zt"], t)
                    turn(psZ, rows[:, u, 0:P], 1).then_inc(s["zt_ps"], 1)

                def parts(t, u, live):
                    es = {d: tn.snap(held[(u - d) % RING], min_val=0, max_val=E - 1) for d in (0, 1, 2) if live(d)}
                    if live(1):
                        pe.wait_ge(s["gated"], t)
                        wait_past(pe, s["gated_sb"], t - 1)
                        turn(psG, gated[:, (u - 1) % 2], 2).then_inc(s["gated_t"], 1)
                    if live(0):
                        pe.wait_ge(s["zt"], t + 1)
                        wait_past(pe, s["gated"], t)
                        product(psU, zt[:, u % 2], es[0], [m.w12], 0, 2 * F1, s["up"])
                    if live(-1):
                        fetch_expert(t + 1, (u + 1) % RING)
                    if live(2):
                        pe.wait_ge(s["act"], t - 1)
                        wait_past(pe, s["act_sb"], t - 2)
                        turn(psA, acts[:, u % 2], 2).then_inc(s["act_t"], 1)
                    if live(-1):
                        turn_rows(t + 1, (u + 1) % RING)
                    if live(1):
                        pe.wait_ge(s["gated_sb"], t)
                        wait_past(pe, s["act"], t - 1)
                        product(psM, gated_t[:, (u - 1) % 2], es[1], [m.wg[:, 0], m.wg[:, 1]], 2 * F1, F1, s["mix"])
                    if live(2):
                        pe.wait_ge(s["act_sb"], t - 1)
                        wait_past(pe, s["out"], t - 2)
                        product(psD, acts_t[:, u % 2], es[2], [m.w3[:, 0], m.w3[:, 1]], 3 * F1, P, s["down"])

                fetch_expert(0, 0)
                turn_rows(0, 0)
                n = SLOT_TILES // RING
                for u in range(RING):
                    parts(u, u, lambda d, t=u: t - d >= 0)
                with pe.Fori(1, n - 1) as i:
                    for u in range(RING):
                        parts(i * RING + u, u, lambda d: True)
                for t in range(SLOT_TILES - RING, SLOT_TILES + 2):
                    parts(t, t % RING, lambda d, t=t: t - d < SLOT_TILES)

            @block.scalar
            def _(act):
                a = nc.scalar

                def take_rows(t, u):
                    act.wait_ge(s["zt_ps"], t + 1)
                    wait_past(act, s["up"], t - 1)
                    a.activation(zt[:, u % 2], psZ, ACT.Copy).then_inc(s["zt"], 1)

                def parts(t, u, live):
                    if live(0):
                        act.wait_ge(s["up"], t + 1)
                        wait_past(act, s["gated"], t - 1)
                        a.activation(x1[:, u % 2], psU[:, 0:F1], ACT.Copy).then_inc(s["x1"], 1)
                    if live(-1):
                        take_rows(t + 1, (u + 1) % RING)
                    if live(1):
                        act.wait_ge(s["mix"], t)
                        wait_past(act, s["act_t"], t - 2)
                        a.activation(acts[:, (u - 1) % 2], psM, ACT.Silu).then_inc(s["act"], 1)
                    if live(2):
                        act.wait_ge(s["down"], t - 1)
                        wait_past(act, s[f"sent{u % 2}"], sent_count(t, u, 4))
                        a.activation(out[:, u % 2], psD, ACT.Copy, scale=rows[:, (u - 2) % RING, P:P + 1]).then_inc(s["out"], 1)

                take_rows(0, 0)
                n = SLOT_TILES // RING
                for u in range(RING):
                    parts(u, u, lambda d, t=u: t - d >= 0)
                with act.Fori(1, n - 1) as i:
                    for u in range(RING):
                        parts(i * RING + u, u, lambda d: True)
                for t in range(SLOT_TILES - RING, SLOT_TILES + 2):
                    parts(t, t % RING, lambda d, t=t: t - d < SLOT_TILES)

            @block.vector
            def _(dve):
                v = nc.vector

                def parts(t, u, live):
                    if live(1):
                        dve.wait_ge(s["gated_t"], t)
                        wait_past(dve, s["mix"], t - 2)
                        v.tensor_copy(gated_t[:, (u - 1) % 2], psG).then_inc(s["gated_sb"], 1)
                    if live(0):
                        dve.wait_ge(s["x1"], t + 1)
                        wait_past(dve, s["gated_t"], t - 1)
                        v.tensor_tensor(gated[:, u % 2], x1[:, u % 2], psU[:, F1:2 * F1], ALU.mult).then_inc(s["gated"], 1)
                    if live(2):
                        dve.wait_ge(s["act_t"], t - 1)
                        wait_past(dve, s["down"], t - 3)
                        v.tensor_copy(acts_t[:, u % 2], psA).then_inc(s["act_sb"], 1)
                each(dve, parts, 2)

            @block.gpsimd
            def _(pool):
                last_row = nc.gpsimd.to_reg(2 * TOKENS - 1)

                def parts(t, u, live):
                    if live(0):
                        pool.wait_ge(s["out"], t + 1)
                        pool.sem_inc(s["taken"], 1)
                        pool.indirect_dma_start(
                            results, bass.IndirectOffsetOnAxis(ap=rows.bitcast(I32)[:, u, P + 1:P + 2], axis=0),
                            out[:, u % 2], None, bounds_check=last_row, oob_is_err=False).then_inc(s[f"sent{u % 2}"], 16)
                each(pool, parts, 0)
                for k in range(2):
                    pool.wait_ge(s[f"sent{k}"], SLOT_TILES // 2 * 16)


def combine(nc, m, name, results):
    with ExitStack() as ctx:
        s = semaphores(nc, ctx, name, "loaded0 loaded1 added")
        take = m.layout()
        got = take(2, GT * 2, P)
        half = results.rearrange("(c t p) d -> c p t d", c=2, p=P)
        with nc.Block() as block:
            @block.sync
            def _(sp):
                def body(i):
                    for c in range(2):
                        wait_past(sp, s["added"], i * 2 + c - 1)
                        sp.dma_start(got[:, c], half[c][:, bass.ds(i * 8, 8), :]).then_inc(s[f"loaded{c}"], 16)
                loop(sp, TILES // 8, body)

            @block.vector
            def _(dve):
                def body(i):
                    for c in range(2):
                        dve.wait_ge(s[f"loaded{c}"], i * 16 + 16)
                        wait_past(dve, s["added"], i * 2 + c)
                        xs = m.x[:, bass.ds(i * 8, 8), :]
                        nc.vector.tensor_tensor(xs, xs, got[:, c], ALU.add).then_inc(s["added"], 1)
                loop(dve, TILES // 8, body)


def state_mix(nc, m, name):
    with ExitStack() as ctx:
        s = semaphores(nc, ctx, name, "scaled shifted z zt_ps zt q_ps v_ps g_ps silu vt state y y_ps yt")
        take = m.layout()
        gates = take(TILES * P)
        z, zt = take(2, GT, P), take(2, GN)
        vt, state, y = take(2, GN), take(2, GN), take(2, GN)
        psT = [m.ps[:, u, :] for u in range(2)]
        psQ, psV, psG = [[m.ps[:, k + 0, :]] * 2 for k in (2, 3, 4)]
        psY = [m.ps[:, 5 + u, :] for u in range(2)]
        decay = m.col("s_decay").to_broadcast([P, T])
        with nc.Block() as block:
            @block.gpsimd
            def _(pool):
                loop(pool, GROUPS // 2, lambda i: [normed(nc, pool, m, s, i * 2 + u, u, m.x, None, z) for u in range(2)])

            @block.tensor
            def _(pe):
                t = nc.tensor

                def back(n, u):
                    pe.wait_ge(s["y"], n + 1)
                    wait_past(pe, s["yt"], n - 1)
                    for k in range(GT):
                        last = t.transpose(psY[u][:, k * P:(k + 1) * P], y[:, u, k * P:(k + 1) * P], m.const("ident"))
                    last.then_inc(s["y_ps"], 1)

                def body(i):
                    for u in range(2):
                        n = i * 2 + u
                        turned(nc, pe, m, s, n, u, z, psT)
                        pe.wait_ge(s["zt"], n + 1)
                        wait_past(pe, s["vt"], n)
                        t.matmul(psV[u], m.mat("s_WvT"), zt[:, u], start=True, stop=True).then_inc(s["v_ps"], 1)
                        wait_past(pe, s["silu"], n)
                        t.matmul(psG[u], m.mat("s_WgT"), zt[:, u], start=True, stop=True).then_inc(s["g_ps"], 1)
                        wait_past(pe, s["y"], n)
                        t.matmul(psQ[u], m.mat("s_WqT"), zt[:, u], start=True, stop=True).then_inc(s["q_ps"], 1)
                        if not (isinstance(n, int) and n == 0):
                            back(n - 1, 1 - u)
                loop(pe, GROUPS // 2, body)
                back(GROUPS - 1, 1)

            @block.scalar
            def _(act):
                a = nc.scalar

                def back(n, u):
                    act.wait_ge(s["y_ps"], n + 1)
                    a.activation(m.xi[:, tiles_of(n), :], psY[u].rearrange("p (t c) -> p t c", t=GT), ACT.Copy)\
                        .then_inc(s["yt"], 1)

                def body(i):
                    for u in range(2):
                        n = i * 2 + u
                        act.wait_ge(s["zt_ps"], n + 1)
                        wait_past(act, s["q_ps"], n - 1)
                        a.activation(zt[:, u], psT[u], ACT.Copy).then_inc(s["zt"], 1)
                        act.wait_ge(s["v_ps"], n + 1)
                        wait_past(act, s["state"], 2 * n - 2)
                        a.activation(vt[:, u], psV[u], ACT.Copy).then_inc(s["vt"], 1)
                        act.wait_ge(s["g_ps"], n + 1)
                        a.activation(gates[:, bass.ds(n * GN, GN)], psG[u], ACT.Silu).then_inc(s["silu"], 1)
                        if not (isinstance(n, int) and n == 0):
                            back(n - 1, 1 - u)
                loop(act, GROUPS // 2, body)
                back(GROUPS - 1, 1)

            @block.vector
            def _(dve):
                v = nc.vector

                def body(i):
                    for u in range(2):
                        n = i * 2 + u
                        dve.wait_ge(s["vt"], n + 1)
                        wait_past(dve, s["y"], n - 1)
                        for b in range(2):
                            v.tensor_tensor_scan(state[:, u, b * T:(b + 1) * T], decay, vt[:, u, b * T:(b + 1) * T],
                                                 0.0, ALU.mult, ALU.add).then_inc(s["state"], 1)
                        dve.wait_ge(s["q_ps"], n + 1)
                        dve.wait_ge(s["state"], 2 * n + 2)
                        wait_past(dve, s["y_ps"], n - 1)
                        v.tensor_tensor(y[:, u], psQ[u], state[:, u], ALU.mult).then_inc(s["y"], 1)
                loop(dve, GROUPS // 2, body)


def state_out(nc, m, name):
    with ExitStack() as ctx:
        s = semaphores(nc, ctx, name, "scaled shifted z zt_ps zt mixed y_ps added")
        take = m.layout()
        gates = take(TILES * P)
        z, zt, y = take(2, GT, P), take(2, GN), take(2, GN)
        psT = [m.ps[:, u, :] for u in range(2)]
        psY = [m.ps[:, 2 + u, :] for u in range(2)]
        with nc.Block() as block:
            @block.gpsimd
            def _(pool):
                loop(pool, GROUPS // 2, lambda i: [normed(nc, pool, m, s, i * 2 + u, u, m.xi, None, z) for u in range(2)])

            @block.tensor
            def _(pe):
                t = nc.tensor

                def body(i):
                    for u in range(2):
                        n = i * 2 + u
                        turned(nc, pe, m, s, n, u, z, psT)
                        pe.wait_ge(s["mixed"], n + 1)
                        wait_past(pe, s["added"], n - 1)
                        for k in range(GT):
                            last = t.matmul(psY[u][:, k * P:(k + 1) * P], y[:, u, k * P:(k + 1) * P], m.mat("s_WoT"),
                                            start=True, stop=True)
                        last.then_inc(s["y_ps"], 1)
                loop(pe, GROUPS // 2, body)

            @block.scalar
            def _(act):
                def body(i):
                    for u in range(2):
                        n = i * 2 + u
                        act.wait_ge(s["zt_ps"], n + 1)
                        wait_past(act, s["mixed"], n - 1)
                        nc.scalar.activation(zt[:, u], psT[u], ACT.Identity, bias=m.col("s_beta"), scale=m.col("s_gamma"))\
                            .then_inc(s["zt"], 1)
                loop(act, GROUPS // 2, body)

            @block.vector
            def _(dve):
                v = nc.vector

                def body(i):
                    for u in range(2):
                        n = i * 2 + u
                        dve.wait_ge(s["zt"], n + 1)
                        wait_past(dve, s["y_ps"], n - 1)
                        v.tensor_tensor(y[:, u], zt[:, u], gates[:, bass.ds(n * GN, GN)], ALU.mult).then_inc(s["mixed"], 1)
                        dve.wait_ge(s["y_ps"], n + 1)
                        xs = m.x[:, tiles_of(n), :]
                        v.tensor_tensor(xs, psY[u].rearrange("p (t c) -> p t c", t=GT), xs, ALU.add).then_inc(s["added"], 1)
                loop(dve, GROUPS // 2, body)


def first_ffn(nc, m, dram, name):
    norm_stats(nc, m, name + "_norm1", m.x, twice=True)
    attention_operands(nc, m, name + "_qkv", (m.mat("f_Wq"), m.mat("f_Wk"), m.mat("f_Wv")),
                       (m.f_bqk[:, 0:1], m.f_bqk[:, 1:2]), m.f_bv[:, :], dram, twice=True)
    attention(nc, m, name + "_att", m.mat("f_Wo"), dram, False, m.xi)
    r = Routing(m)
    norm_stats(nc, m, name + "_norm2", m.xi)
    gate(nc, m, name + "_gate", r, m.xi, m.f_Wg[:, :], m.f_bg[:, :], None, True)
    choose(nc, m, name + "_choose", r)
    experts_dense(nc, m, name + "_experts", r)


def first_attention(nc, m, dram, name):
    norm_stats(nc, m, name + "_norm", m.x)
    attention_operands(nc, m, name + "_qkv", (m.mat("a_WqT"), m.mat("a_Wk"), m.mat("a_Wv")),
                       (m.col("a_bq"), m.col("a_bk")), m.row("a_bv"), dram, twice=False)
    attention(nc, m, name + "_att", m.mat("a_Wo"), dram, True, m.x)


def second_ffn(nc, m, dram, name, which):
    r = Routing(m)
    rows = m.arena[:, 0:TILES * 2 * ROW].rearrange("p (t c w) -> p t c w", c=2, w=ROW)
    norm_stats(nc, m, name + "_norm", m.x)
    gate(nc, m, name + "_gate", r, m.x, m.m_Wg[:, :], m.col("m_gate_b")[0:E, :], rows, False)
    choose(nc, m, name + "_choose", r, dispatch=rows)
    scatter(nc, m, name + "_scatter", r, rows, dram["slots"][which])
    experts_routed(nc, m, name + "_experts", r, dram["slots"][which], dram["results"][which])
    combine(nc, m, name + "_combine", dram["results"][which])


def second_attention(nc, m, name):
    norm_stats(nc, m, name + "_norm1", m.x)
    state_mix(nc, m, name + "_mix")
    norm_stats(nc, m, name + "_norm2", m.xi)
    state_out(nc, m, name + "_out")


def build(nc, dram, stages=6):
    with ExitStack() as ctx:
        m = Memory(nc, ctx)
        setup(nc, m, dram)
        steps = [lambda: first_ffn(nc, m, dram, "f1"), lambda: first_attention(nc, m, dram, "a1"),
                 lambda: first_ffn(nc, m, dram, "f2"), lambda: second_ffn(nc, m, dram, "g1", 0),
                 lambda: second_attention(nc, m, "a2"), lambda: second_ffn(nc, m, dram, "g2", 1)]
        for step in steps[:stages]:
            step()
        dump(nc, m, dram, m.x)


def dump(nc, m, dram, src):
    with ExitStack() as ctx:
        s = semaphores(nc, ctx, "out", "stored")
        with nc.Block() as block:
            @block.sync
            def _(sp):
                sp.dma_start(dram["out"].rearrange("(t p) c -> p t c", p=P), src[:, :, :]).then_inc(s["stored"], 16)
                sp.wait_ge(s["stored"], 16)


def kernel(**inputs):
    import numpy as _np
    import concourse.bacc as _bacc
    from concourse import mybir as _mybir
    from concourse.bass_utils import run_bass_kernel_spmd as _run

    a = {k: _np.ascontiguousarray(v) for k, v in inputs.items()}
    f, q, r, e = "L0_ffn_", "L0_attn_", "L1_attn_", "L1_ffn_"
    cols = {
        "f_g1": a[f + "g1"], "f_b1": a[f + "b1"], "f_g2": a[f + "g2"], "f_b2": a[f + "b2"],
        "a_bq": a[q + "bq"], "a_bk": _np.tile(a[q + "bk"], H),
        "s_gamma": a[r + "ln_gamma"], "s_beta": a[r + "ln_beta"], "s_decay": _np.repeat(a[r + "decay"], D),
        "m_gate_b": _np.tile(a[e + "gate_b"], P // E),
    }
    arrays = {
        "x": a[q + "x"].reshape(TOKENS, P),
        "consts": _np.concatenate(list(CONST.values()), 1),
        "cols": _np.ascontiguousarray(_np.stack([cols[n] for n in COLS], 1)),
        "rows": _np.concatenate([_np.tile(a[q + "bv"], H), a[q + "bo"]])[None, :],
        "f_Wq": a[f + "Wq"], "f_Wk": a[f + "Wk"], "f_Wv": a[f + "Wv"], "f_Wo": a[f + "Wo"],
        "f_Wg": a[f + "Wg"], "f_W1": a[f + "W1"], "f_W2": a[f + "W2"],
        "a_WqT": a[q + "Wq"].T, "a_Wk": a[q + "Wk"], "a_Wv": a[q + "Wv"], "a_Wo": a[q + "Wo"],
        "s_WqT": a[r + "Wq"].T, "s_WvT": a[r + "Wv"].T, "s_WgT": a[r + "Wg"].T, "s_WoT": a[r + "Wo"].T,
        "m_Wg": a[e + "gate_w"], "m_w1": a[e + "w1"], "m_w2": a[e + "w2"], "m_wg": a[e + "wg"], "m_w3": a[e + "w3"],
        "m_biases": _np.concatenate([a[e + "b1"], a[e + "b2"], a[e + "bg"], a[e + "b3"]], 1),
    }
    arrays = {"in_" + k: _np.ascontiguousarray(v) for k, v in arrays.items()}
    nc = _bacc.Bacc("TRN2", target_bir_lowering=False, num_devices=1)
    dram = {k[3:]: nc.dram_tensor(k, v.shape, _mybir.dt.from_np(v.dtype), kind="ExternalInput").ap()
            for k, v in arrays.items()}
    dram["out"] = nc.dram_tensor("out", (TOKENS, P), F32, kind="ExternalOutput").ap()
    dram["q_parts"] = nc.dram_tensor("q_parts", (H, 3, D, TOKENS), BF16, kind="Internal").ap()
    dram["k_parts"] = nc.dram_tensor("k_parts", (H, len(PART_K), D, TOKENS), BF16, kind="Internal").ap()
    dram["slots"] = [nc.dram_tensor(f"slots{i}", (SLOTS, ROW), F32, kind="Internal").ap() for i in range(2)]
    dram["results"] = [nc.dram_tensor(f"results{i}", (2 * TOKENS, P), F32, kind="Internal").ap() for i in range(2)]
    build(nc, dram)
    got = _run(nc, [arrays], core_ids=[0])
    return got.results[0]["out"].reshape(B, T, P)
```

```python
from contextlib import ExitStack

import numpy as np
import concourse.bass as bass
from concourse import mybir

F32 = mybir.dt.float32
BF16 = mybir.dt.bfloat16
I32 = mybir.dt.int32
ALU = mybir.AluOpType
ACT = mybir.ActivationFunctionType
AX = mybir.AxisListType

P = 128
B, T = 16, 256
TILES = B * T // P
GT = 4
GROUPS = TILES // GT
GN = GT * P
H, D = 16, 8
QH = 4
QUADS = H // QH
E, K0 = 8, 64
CH = E * K0 // P
F1 = 256
TOKENS = B * T
SLOT_TILES = 2 * TOKENS // P + E
SLOTS = SLOT_TILES * P
RING = 8
ROW = P + 2
LATE = 6 + 2 * 4
ARENA = 21500
NOWHERE = 1 << 20
EPS = 1e-5
SCALE = float(D) ** -0.5
MASKED = -1e30

PART_Q = [0, 1, 2, 0, 1, 0]
PART_K = [0, 0, 0, 1, 1, 2]
SPLIT_ROWS = D * len(PART_Q)
SHIFT_ROW = 96


def constants():
    ident = np.eye(P, dtype=np.float32)
    perm = np.zeros((D, D), np.float32)
    for out, src in enumerate([0, 2, 1, 3, 4, 6, 5, 7]):
        perm[out, src] = 1.0
    half = D // 2
    theta = (np.float32(1.0) / np.float32(10000.0) ** (np.arange(0, half, 2, dtype=np.float32) / np.float32(half)))
    rope = np.zeros((P, P), np.float32)
    for h in range(H):
        rot = np.zeros((D, D), np.float32)
        freq = (np.float32(h) * theta).astype(np.float32)
        for x in range(2):
            for n in range(2):
                even, odd = half * x + 2 * n, half * x + 2 * n + 1
                rot[half * x + n, even], rot[half * x + n, odd] = np.cos(freq[n]), -np.sin(freq[n])
                rot[half * x + 2 + n, even], rot[half * x + 2 + n, odd] = np.sin(freq[n]), np.cos(freq[n])
        rope[h * D:(h + 1) * D, h * D:(h + 1) * D] = rot.T @ perm
    row, column = np.arange(P)[:, None], np.arange(P)[None, :]
    mask = np.where(column <= row, 0.0, MASKED).astype(np.float32)
    sel = np.zeros((P, CH * P), np.float32)
    for m in range(CH * P):
        for k in range(3):
            sel[k * E + m // K0, m] = 1.0
    before = (row < column).astype(np.float32)
    rev = np.tile(np.arange(E, 0, -1, dtype=np.float32), (P, 1))
    return {
        "ident": ident, "rope": rope,
        "mask_rows": mask, "mask_cols": mask.T,
        "sel": sel, "before": before, "rev": rev,
        "eps": np.full((P, 1), EPS, np.float32),
        "slot": np.tile(np.arange(SLOT_TILES, dtype=np.float32), (P, 1)),
        "token": (np.arange(TILES)[None, :] * P + np.arange(P)[:, None]).astype(np.float32),
    }


CONST = constants()
CONST_AT, _at = {}, 0
for _n, _a in CONST.items():
    CONST_AT[_n] = (_at, _a.shape[1])
    _at += _a.shape[1]
CONST_COLS = _at

COLS = ["f_g1", "f_b1", "f_g2", "f_b2", "a_bq", "a_bk", "s_gamma", "s_beta", "s_decay", "m_gate_b"]
ROWS = {"a_bv": P, "a_bo": P}
ROW_AT, _at = {}, 0
for _n, _w in ROWS.items():
    ROW_AT[_n] = (_at, _w)
    _at += _w
ROW_COLS = _at
MATS = ["f_Wq", "f_Wk", "f_Wv", "f_Wo", "a_WqT", "a_Wk", "a_Wv", "a_Wo", "s_WqT", "s_WvT", "s_WgT", "s_WoT"]


class Memory:

    def __init__(self, nc, ctx):
        self.nc, self.ctx = nc, ctx
        self.cst = self.keep("cst", [P, CONST_COLS])
        self.x = self.keep("x", [P, TILES, P])
        self.xi = self.keep("xi", [P, TILES, P])
        self.cols = self.keep("cols", [P, len(COLS)])
        self.rows = self.keep("rows", [P, ROW_COLS])
        self.mats = self.keep("mats", [P, len(MATS), P])
        self.identb = self.keep("identb", [P, P], BF16)
        self.selb = self.keep("selb", [P, CH * P], BF16)
        self.maskb = self.keep("maskb", [P, 2, P], BF16)
        self.f_W1 = self.keep("f_W1", [P, CH, P])
        self.f_W2 = self.keep("f_W2", [P, CH, P])
        self.f_Wg = self.keep("f_Wg", [P, E])
        self.f_bqk = self.keep("f_bqk", [P, 2])
        self.f_bv = self.keep("f_bv", [P, P])
        self.f_bg = self.keep("f_bg", [E, 1])
        self.f_bh = self.keep("f_bh", [P, CH])
        self.st = self.keep("st", [P, TILES, 6])
        self.stats = {n: self.keep(n, [P, TILES]) for n in
                      "total apart both mean var sd rstd nmr ratio sd2 rstd2".split()}
        self.w12 = self.keep("w12", [P, E, 2 * F1])
        self.wg = self.keep("wg", [P, 2, E, F1])
        self.w3 = self.keep("w3", [P, 2, E, P])
        self.m_Wg = self.keep("m_Wg", [P, E])
        self.bias3 = self.keep("bias3", [P, E, 3 * F1 + P], BF16)
        self.ones3 = self.keep("ones3", [P, P], BF16)
        self.arena = self.keep("arena", [P, ARENA])
        self.empty = self.keep("empty", [P, ROW])
        self.late = nc.alloc_semaphore("late")
        self.ps = ctx.enter_context(nc.psum_tensor("ps", [P, 8, 512], F32))

    def keep(self, name, shape, dt=F32):
        return self.ctx.enter_context(self.nc.sbuf_tensor(name, shape, dt))

    def const(self, name):
        at, n = CONST_AT[name]
        return self.cst[:, at:at + n]

    def col(self, name):
        n = COLS.index(name)
        return self.cols[:, n:n + 1]

    def row(self, name):
        at, n = ROW_AT[name]
        return self.rows[:, at:at + n]

    def mat(self, name):
        return self.mats[:, MATS.index(name), :]

    def layout(self):
        at = [0]

        def take(*shape, dt=F32):
            n = int(np.prod(shape))
            words = n if dt != BF16 else (n + 1) // 2
            flat = self.arena[:, at[0]:at[0] + words]
            at[0] += words
            assert at[0] <= ARENA, at[0]
            if dt != F32:
                flat = flat.bitcast(dt)
            if len(shape) == 1:
                return flat
            names = "abcdef"[:len(shape)]
            return flat.rearrange(f"p ({' '.join(names)}) -> p {' '.join(names)}",
                                  **{n: s for n, s in zip(names[1:], shape[1:])})
        return take


def semaphores(nc, ctx, prefix, names):
    made = {n: nc.alloc_semaphore(f"{prefix}_{n}") for n in names.split()}
    ctx.callback(nc.all_engine_barrier)
    ctx.callback(nc.clear_and_free_semaphores, list(made.values()))
    return made


def wait_past(eng, sem, count):
    if not (isinstance(count, int) and count <= 0):
        eng.wait_ge(sem, count)


def loop(eng, n, body):
    body(0)
    with eng.Fori(1, n) as i:
        body(i)


def steps(eng, part, lead=0):
    for n in range(-lead, 2):
        part(n // 2, n % 2, lambda d, n=n: n + d >= 0)
    with eng.Fori(1, GROUPS // 2 - 1) as i:
        for u in range(2):
            part(i, u, lambda d: True)
    for n in range(GROUPS - 2, GROUPS):
        part(n // 2, n % 2, lambda d, n=n: n + d < GROUPS)


def setup(nc, m, dram):
    with ExitStack() as ctx:
        s = semaphores(nc, ctx, "setup", "loaded spread pe split link parts filled rows_ready")
        take = m.layout()
        w1_raw, wg_raw, b1s, wk8, wv8 = take(E, K0), take(E), take(P), take(D), take(D)
        BW = 3 * F1 + P
        bias_raw, bias_rest = take(BW), take(BW)
        bias_parts = take(3, BW, dt=BF16)
        empty, late = m.empty[:, :], m.late
        LOADS = 12 + len(MATS)
        with nc.Block() as block:
            @block.sync
            def _(sp):
                def load(dst, src):
                    sp.dma_start(dst, src).then_inc(s["loaded"], 16)
                load(m.cst[:, :], dram["consts"])
                load(m.cols[:, :], dram["cols"])
                load(m.rows[:, :], dram["rows"].to_broadcast([P, ROW_COLS]))
                load(m.x[:, :, :], dram["x"].rearrange("(t p) c -> p t c", p=P))
                load(m.f_W2[:, :, :], dram["f_W2"].rearrange("e k d -> (e k) d").rearrange("(c p) d -> p c d", p=P))
                sp.wait_ge(s["parts"], 3)
                sp.wait_ge(s["rows_ready"], 1)
                for k in range(3):
                    sp.dma_start(m.bias3[k:k + 1, :, :], bias_parts[0:E, k]).then_inc(s["filled"], 16)
                sp.wait_ge(s["filled"], 16 * 3)
                sp.wait_ge(s["loaded"], 16 * LOADS)

            @block.scalar
            def _(act):
                def load(dst, src):
                    act.dma_start(dst, src).then_inc(s["loaded"], 16)
                load(w1_raw, dram["f_W1"].rearrange("e d k -> d e k"))
                load(wg_raw, dram["f_Wg"])
                load(m.m_Wg[:, :], dram["m_Wg"])
                load(wk8, dram["a_Wk"])
                load(wv8, dram["a_Wv"])
                load(bias_raw[0:E], dram["m_biases"])
                load(b1s[0:1, :], dram["rows"][:, 0:P])
                for n in MATS:
                    load(m.mat(n), dram["f_Wk" if n in ("a_Wk", "a_Wv") else n])
                act.wait_ge(s["loaded"], 16 * LOADS)
                act.wait_ge(s["filled"], 16 * 3)

                def load_late(dst, src):
                    act.dma_start(dst, src).then_inc(late, 16)
                load_late(m.w12[:, :, 0:F1], dram["m_w1"].rearrange("e p f -> p e f"))
                load_late(m.w12[:, :, F1:2 * F1], dram["m_w2"].rearrange("e p f -> p e f"))
                for k in range(2):
                    load_late(m.wg[:, k], dram["m_wg"][:, k * P:(k + 1) * P, :].rearrange("e p f -> p e f"))
                    load_late(m.w3[:, k], dram["m_w3"][:, k * P:(k + 1) * P, :].rearrange("e p f -> p e f"))
                act.wait_ge(s["rows_ready"], 3)
                for d in dram["slots"]:
                    for q in range(4):
                        n = SLOTS // 4
                        load_late(d[q * n:(q + 1) * n, :].rearrange("(t p) c -> p t c", p=P),
                                  empty.unsqueeze(1).to_broadcast([P, SLOT_TILES // 4, ROW]))

            @block.gpsimd
            def _(pool):
                g = nc.gpsimd
                g.memset(m.ones3[:, :], 1.0)
                g.memset(m.bias3[:, :, :].rearrange("p e n -> p (e n)").bitcast(F32), 0.0).then_inc(s["rows_ready"], 1)
                g.memset(empty[:, 0:P + 1], 0.0).then_inc(s["rows_ready"], 1)
                g.memset(empty.bitcast(I32)[:, P + 1:P + 2], NOWHERE).then_inc(s["rows_ready"], 1)

            @block.tensor
            def _(pe):
                t, ps = nc.tensor, m.ps
                pe.wait_ge(s["loaded"], 16 * LOADS)
                pe.wait_ge(s["link"], 1)
                t.matmul(ps[:, 0, 0:1], m.mat("f_Wq"), m.col("f_b1"), start=True, stop=True)
                t.matmul(ps[:, 0, 1:2], m.mat("f_Wk"), m.col("f_b1"), start=True, stop=True)
                for c in range(CH):
                    t.matmul(ps[:, 0, 2 + c:3 + c], w1_raw[:, 2 * c:2 * c + 2, :].rearrange("p e k -> p (e k)"),
                             m.col("f_b2"), start=True, stop=True)
                t.matmul(ps[0:E, 0, 9:10], wg_raw, m.col("f_b2"), start=True, stop=True)
                t.matmul(ps[:, 1, 0:P], m.mat("a_WqT"), m.const("rope"), start=True, stop=True)
                t.matmul(ps[:, 0, 8:9], m.const("rope"), m.col("a_bq"), start=True, stop=True)
                pe.wait_ge(s["spread"], 1)
                t.matmul(ps[:, 2, 0:P], b1s, m.mat("f_Wv"), start=True, stop=True).then_inc(s["pe"], 1)

            @block.vector
            def _(dve):
                v, ps = nc.vector, m.ps
                v.memset(ps[:, :, :], 0.0).then_inc(s["link"], 1)
                dve.wait_ge(s["loaded"], 16 * LOADS)
                v.tensor_copy(b1s, m.col("f_b1").to_broadcast([P, P])).then_inc(s["spread"], 1)
                v.tensor_copy(m.identb[:, :], m.const("ident"))
                v.tensor_copy(m.selb[:, :], m.const("sel"))
                v.tensor_copy(m.maskb[:, 0], m.const("mask_rows"))
                v.tensor_copy(m.maskb[:, 1], m.const("mask_cols"))
                v.tensor_copy(m.mat("a_Wk").rearrange("p (h d) -> p h d", h=H), wk8.unsqueeze(1).to_broadcast([P, H, D]))
                v.tensor_copy(m.mat("a_Wv").rearrange("p (h d) -> p h d", h=H), wv8.unsqueeze(1).to_broadcast([P, H, D]))
                one = slice(0, E)
                v.tensor_copy(bias_parts[one, 0], bias_raw[one]).then_inc(s["parts"], 1)
                dve.wait_ge(s["parts"], 1)
                v.tensor_tensor(bias_rest[one], bias_raw[one], bias_parts[one, 0], ALU.subtract).then_inc(s["split"], 1)
                dve.wait_ge(s["split"], 1)
                v.tensor_copy(bias_parts[one, 1], bias_rest[one]).then_inc(s["parts"], 1)
                dve.wait_ge(s["parts"], 2)
                v.tensor_tensor(bias_parts[one, 2], bias_rest[one], bias_parts[one, 1], ALU.subtract).then_inc(s["parts"], 1)
                dve.wait_ge(s["pe"], 1)
                v.tensor_copy(m.f_bqk[:, :], ps[:, 0, 0:2])
                v.tensor_copy(m.f_bh[:, :], ps[:, 0, 2:2 + CH])
                v.tensor_copy(m.f_bg[:, :], ps[0:E, 0, 9:10])
                v.tensor_copy(m.col("a_bq"), ps[:, 0, 8:9])
                v.tensor_copy(m.mat("a_WqT"), ps[:, 1, 0:P])
                v.tensor_copy(m.f_bv[:, :], ps[:, 2, 0:P])
                for w in ("f_Wq", "f_Wk", "f_Wv"):
                    v.tensor_scalar(m.mat(w), m.mat(w), m.col("f_g1"), None, ALU.mult)
                v.tensor_scalar(m.f_W1[:, :, :].rearrange("p c k -> p (c k)"), w1_raw.rearrange("p e k -> p (e k)"),
                                m.col("f_g2"), None, ALU.mult)
                v.tensor_scalar(m.f_Wg[:, :], wg_raw, m.col("f_g2"), None, ALU.mult)


NORM = "stats summed squared var sqrt rstd nmr once ratio sqrt2 rstd2 scaled shifted z "


HALVES = (slice(0, 2 * GT), slice(2 * GT, TILES))


def norm_stats(nc, dve, m, s, i, src, twice=False):
    v, half = nc.vector, HALVES[i]
    c = {n: a[:, half] for n, a in m.stats.items()}
    st = m.st[:, half, :]
    for t in range(half.start, half.stop):
        v.bn_stats(m.st[:, t, :], src[:, t, :]).then_inc(s["stats"], 1)
    dve.wait_ge(s["stats"], half.stop)
    v.tensor_tensor(c["total"], st[:, :, 1], st[:, :, 4], ALU.add)
    v.tensor_tensor(c["both"], st[:, :, 2], st[:, :, 5], ALU.add)
    v.tensor_tensor(c["apart"], st[:, :, 1], st[:, :, 4], ALU.subtract).then_inc(s["summed"], 1)
    dve.wait_ge(s["summed"], i + 1)
    v.scalar_tensor_tensor(out=c["apart"], in0=c["apart"], scalar=0.25, in1=c["apart"], op0=ALU.mult, op1=ALU.mult)\
        .then_inc(s["squared"], 1)
    dve.wait_ge(s["squared"], i + 1)
    v.scalar_tensor_tensor(out=c["var"], in0=c["both"], scalar=1.0 / P, in1=c["apart"], op0=ALU.mult, op1=ALU.add)\
        .then_inc(s["var"], 1)
    dve.wait_ge(s["sqrt"], i + 1)
    v.reciprocal(c["rstd"], c["sd"]).then_inc(s["rstd"], 1)
    dve.wait_ge(s["rstd"], i + 1)
    v.scalar_tensor_tensor(out=c["nmr"], in0=c["total"], scalar=-0.5, in1=c["rstd"], op0=ALU.mult, op1=ALU.mult)\
        .then_inc(s["nmr"], 1)
    if twice:
        v.tensor_tensor(c["ratio"], c["var"], c["rstd"], ALU.mult).then_inc(s["once"], 1)
        dve.wait_ge(s["once"], i + 1)
        v.tensor_tensor(c["ratio"], c["ratio"], c["rstd"], ALU.mult).then_inc(s["ratio"], 1)
        dve.wait_ge(s["sqrt2"], i + 1)
        v.reciprocal(c["rstd2"], c["sd2"]).then_inc(s["rstd2"], 1)


def norm_roots(nc, act, m, s, i, twice=False):
    for src, out, ready, done in (("var", "sd", "var", "sqrt"), ("ratio", "sd2", "ratio", "sqrt2"))[:2 if twice else 1]:
        act.wait_ge(s[ready], i + 1)
        nc.scalar.activation(m.stats[out][:, HALVES[i]], m.stats[src][:, HALVES[i]], ACT.Sqrt, bias=m.const("eps")).then_inc(s[done], 1)
def spread(cols, n):
    return cols[:, bass.ds(n * GT, GT)].unsqueeze(2).to_broadcast([P, GT, P])


def tiles_of(n):
    return bass.ds(n * GT, GT)


def normed(nc, pool, m, s, i, u, src, keep, z):
    g, n = nc.gpsimd, i * 2 + u
    out = z[:, u] if keep is None else keep[:, tiles_of(n), :]
    if keep is None:
        wait_past(pool, s["zt_ps"], n - 1)
    half = 1 if isinstance(i, int) and i == 0 else 2
    pool.wait_ge(s["nmr"], half)
    g.tensor_tensor(out, src[:, tiles_of(n), :], spread(m.stats["rstd"], n), ALU.mult).then_inc(s["scaled"], 1)
    pool.wait_ge(s["scaled"], n + 1)
    g.tensor_tensor(out, out, spread(m.stats["nmr"], n), ALU.add).then_inc(s["z" if keep is None else "shifted"], 1)
    if keep is not None:
        pool.wait_ge(s["rstd2"], half)
        pool.wait_ge(s["shifted"], n + 1)
        wait_past(pool, s["zt_ps"], n - 1)
        g.tensor_tensor(z[:, u], out, spread(m.stats["rstd2"], n), ALU.mult).then_inc(s["z"], 1)


def turned(nc, pe, m, s, n, u, z, psT):
    pe.wait_ge(s["z"], n + 1)
    wait_past(pe, s["zt"], n - 1)
    for k in range(GT):
        last = nc.tensor.transpose(psT[u][:, k * P:(k + 1) * P], z[:, u, k, :], m.const("ident"))
    last.then_inc(s["zt_ps"], 1)


def attention_operands(nc, m, name, weights, biases, v_bias, dram, twice):
    Wq, Wk, Wv = weights
    with ExitStack() as ctx:
        s = semaphores(nc, ctx, name, NORM + "zt_ps zt q_ps k_ps v_ps top rest mid low v stored")
        take = m.layout()
        val = take(TILES, H, D + 1)
        z = take(2, GT, P)
        zt = take(2, GN)
        parts = take(2, 3, TOKENS, dt=BF16)
        rest = take(2, 2, GN)
        psT = [m.ps[:, u, :] for u in range(2)]
        psQK = [[m.ps[:, 2 + 2 * u + w, :] for w in range(2)] for u in range(2)]
        psV = [m.ps[:, 6 + u, :] for u in range(2)]

        def place(n, w, k):
            return parts[:, w, k, bass.ds(n * GN, GN)]

        with nc.Block() as block:
            @block.gpsimd
            def _(pool):
                g = nc.gpsimd
                g.memset(val[:, :, :, D], 1.0)

                def body(i):
                    for u in range(2):
                        n = i * 2 + u
                        normed(nc, pool, m, s, i, u, m.x, m.xi if twice else None, z)
                        if not twice:
                            g.tensor_tensor(m.x[:, tiles_of(n), :], m.x[:, tiles_of(n), :],
                                            m.row("a_bo").unsqueeze(1).to_broadcast([P, GT, P]), ALU.add)
                loop(pool, GROUPS // 2, body)

            @block.tensor
            def _(pe):
                t = nc.tensor

                def project(n, u):
                    pe.wait_ge(s["zt"], n + 1)
                    wait_past(pe, s["rest"], 2 * n - 3)
                    t.matmul(psQK[u][0], Wq, zt[:, u], start=True, stop=True).then_inc(s["q_ps"], 1)
                    wait_past(pe, s["rest"], 2 * n - 2)
                    t.matmul(psQK[u][1], Wk, zt[:, u], start=True, stop=True).then_inc(s["k_ps"], 1)
                    wait_past(pe, s["v"], n - 1)
                    for k in range(GT):
                        last = t.matmul(psV[u][:, k * P:(k + 1) * P], zt[:, u, k * P:(k + 1) * P], Wv,
                                        start=True, stop=True)
                    last.then_inc(s["v_ps"], 1)

                def part(i, u, live):
                    n = i * 2 + u
                    if live(1):
                        turned(nc, pe, m, s, n + 1, 1 - u, z, psT)
                    if live(0):
                        project(n, u)
                steps(pe, part, 1)

            @block.scalar
            def _(act):
                a = nc.scalar

                def part(i, u, live):
                    n = i * 2 + u
                    if live(1):
                        act.wait_ge(s["zt_ps"], n + 2)
                        wait_past(act, s["v_ps"], n)
                        a.activation(zt[:, 1 - u], psT[1 - u], ACT.Copy).then_inc(s["zt"], 1)
                    if not live(0):
                        norm_roots(nc, act, m, s, 1, twice)
                    if live(0):
                        for w, ready in enumerate(("q_ps", "k_ps")):
                            act.wait_ge(s[ready], n + 1)
                            a.activation(place(n, w, 0), psQK[u][w], ACT.Identity, bias=biases[w])\
                                .then_inc(s["top"], 1)
                norm_roots(nc, act, m, s, 0, twice)
                steps(act, part, 1)

            @block.vector
            def _(dve):
                v = nc.vector

                def split(n, u):
                    for w in range(2):
                        dve.wait_ge(s["top"], 2 * n + w + 1)
                        v.scalar_tensor_tensor(out=rest[:, u, w], in0=psQK[u][w], scalar=biases[w],
                                               in1=place(n, w, 0), op0=ALU.add, op1=ALU.subtract)\
                            .then_inc(s["rest"], 1)
                        dve.wait_ge(s["rest"], 2 * n + w + 1)
                        v.tensor_copy(place(n, w, 1), rest[:, u, w]).then_inc(s["mid"], 1)
                    dve.wait_ge(s["v_ps"], n + 1)
                    for k in range(GT):
                        last = v.tensor_tensor(val[:, n * GT + k, :, 0:D],
                                               psV[u][:, k * P:(k + 1) * P].rearrange("p (h d) -> p h d", h=H),
                                               v_bias.rearrange("p (h d) -> p h d", h=H), ALU.add)
                    last.then_inc(s["v"], 1)
                    for w in range(2):
                        dve.wait_ge(s["mid"], 2 * n + w + 1)
                        v.tensor_tensor(place(n, w, 2), rest[:, u, w], place(n, w, 1), ALU.subtract)\
                            .then_inc(s["low"], 1)

                for half in range(2):
                    norm_stats(nc, dve, m, s, half, m.x, twice)
                steps(dve, lambda i, u, live: split(i * 2 + u, u))

            @block.sync
            def _(sp):
                def store(i):
                    tok = bass.ds(i * 2 * GN, 2 * GN)
                    sp.wait_ge(s["low"], 4 * i + 4)
                    for k in range(3):
                        sp.dma_start(dram["q_parts"][:, k, :, tok], parts[:, 0, k, tok]).then_inc(s["stored"], 16)
                    for r, k in enumerate(PART_K):
                        sp.dma_start(dram["k_parts"][:, r, :, tok], parts[:, 1, k, tok]).then_inc(s["stored"], 16)
                loop(sp, GROUPS // 2, store)
                sp.wait_ge(s["stored"], GROUPS // 2 * (16 * 9))


def attention(nc, m, name, Wo, dram, causal, out):
    LOADS, SHIFTS, RQ = 4, 2, 2 * QUADS
    with ExitStack() as ctx:
        s = semaphores(nc, ctx, name, "zeroed loaded0 loaded1 loaded2 loaded3 row_scores maxed mx_t shift_hi shift_lo "
                       "shifted0 shifted1 col_scores probs vals pv pv_sb ot_ps recip otok otok_t ot proj added")
        loaded = [s[f"loaded{k}"] for k in range(RQ // 2)]
        shifted = [s[f"shifted{c}"] for c in range(2)]
        take = m.layout()
        val = take(TILES, H, D + 1)
        qr = take(RQ, QH, T, dt=BF16)
        kr = take(RQ, QH, T, dt=BF16)
        vals = take(QUADS, 2, QH, D + 1)
        probs = take(2, QH, 2 * T)
        mx = take(2, 2, QH)
        shift = take(2, 2, T, dt=BF16)
        pv_sb = take(2, T)
        rec = take(2, QH)
        otok = take(2, H, D)
        ot = take(T)
        S1 = [m.ps[:, u, :] for u in range(2)]
        S2 = [m.ps[:, 2 + u, :] for u in range(2)]
        PV, FIN, OT = m.ps[:, 4, 0:T], m.ps[:, 5, 0:T], m.ps[:, 6, 0:T]
        MX = m.ps[0:QH, 7, 0:T]
        mask_rows, mask_cols = m.maskb[:, 0], m.maskb[:, 1]
        rows_at = [(0, P), (P, 3 * P)] if causal else [(0, T), (T, 2 * T)]
        cols_at = [(0, T), (T, T + P)] if causal else [(0, T), (T, 2 * T)]

        def at(i, c, ahead):
            i2, c2 = i + (c + ahead) // RQ, (c + ahead) % RQ
            return i2, c2, i2 * RQ + c2

        def quads(eng, slot):
            for c in range(RQ):
                slot(0, c, c, lambda d, c=c: c + d >= 0)
            with eng.Fori(1, B // 2 - 1) as i:
                for c in range(RQ):
                    slot(i, c, i * RQ + c, lambda d: True)
            for c in range(RQ):
                slot(B // 2 - 1, c, (B // 2 - 1) * RQ + c, lambda d, c=c: c + d < RQ)

        def batch(i, c):
            return i * 2 + c // QUADS

        END = at(B // 2 - 1, RQ - 1, 0)

        with nc.Block() as block:
            @block.gpsimd
            def _(pool):
                g = nc.gpsimd
                g.memset(kr[0:SHIFT_ROW].bitcast(F32), 0.0).then_inc(s["zeroed"], 1)

                def slot(i, c, n, live):
                    q = c % QUADS
                    wait_past(pool, s["pv"], n - 3)
                    g.tensor_copy(vals[:, q], val[:, bass.ds(batch(i, c) * 2, 2), QH * q:QH * q + QH, :])\
                        .then_inc(s["vals"], 1)
                quads(pool, slot)

            @block.sync
            def _(sp):
                def load(i, c):
                    q = c % QUADS
                    tok, heads = bass.ds(batch(i, c) * T, T), slice(QH * q, QH * q + 2 * QH)
                    at_row = 0
                    for count in (3, 2, 1):
                        sp.dma_start(qr[at_row:at_row + D * count, c:c + 2].rearrange("p c h t -> p (c h) t"),
                                     dram["q_parts"][heads, 0:count, :, tok].rearrange("h a d t -> (a d) h t"))\
                            .then_inc(loaded[c // 2], 16)
                        at_row += D * count
                    sp.dma_start(kr[0:SPLIT_ROWS, c:c + 2].rearrange("p c h t -> p (c h) t"),
                                 dram["k_parts"][heads, :, :, tok].rearrange("h a d t -> (a d) h t"))\
                        .then_inc(loaded[c // 2], 16)

                def store_shift(i, c, n):
                    sp.wait_ge(s["shift_lo"], n + 1)
                    for k in range(2):
                        sp.dma_start(qr[SHIFT_ROW + k:SHIFT_ROW + k + 1, c], shift[0:QH, c % 2, k])\
                            .then_inc(shifted[c % 2], 16)

                def slot(i, c, n, live):
                    if live(2):
                        store_shift(*at(i, c, 2))
                    if c % 2 == 1 and live(RQ):
                        sp.wait_ge(s["col_scores"], n * QH + QH)
                        load(i + 1, c - 1)

                sp.wait_ge(s["zeroed"], 2)
                for c in range(0, RQ, 2):
                    load(0, c)
                store_shift(0, 0, 0)
                store_shift(0, 1, 1)
                quads(sp, slot)

            @block.tensor
            def _(pe):
                t = nc.tensor

                def row_scores(i, c, n, j):
                    if j == 0 and c % 2 == 0:
                        pe.wait_ge(loaded[c // 2], (i + 1) * (16 * LOADS))
                    wait_past(pe, s["maxed"], n * QH + j - 1)
                    for qt in range(2):
                        o = S1[j % 2][:, rows_at[qt][0]:rows_at[qt][1]]
                        q = qr[0:SHIFT_ROW, c, j, qt * P:(qt + 1) * P]
                        if not causal:
                            last = t.matmul(o, q, kr[0:SHIFT_ROW, c, j], start=True, stop=True)
                        else:
                            if qt == 1:
                                t.matmul(o[:, 0:P], q, kr[0:SHIFT_ROW, c, j, 0:P], start=True, stop=True)
                            o = o[:, qt * P:(qt + 1) * P]
                            t.matmul(o, q, kr[0:SHIFT_ROW, c, j, qt * P:(qt + 1) * P], start=True, stop=False)
                            last = t.matmul(o, m.identb[:, :], mask_rows, start=False, stop=True)
                    last.then_inc(s["row_scores"], 1)

                def col_scores(i, c, n, j):
                    if j == 0:
                        pe.wait_ge(shifted[c % 2], (i * QUADS + c // 2 + 1) * (16 * SHIFTS))
                    wait_past(pe, s["probs"], n * QH + j - 1)
                    for kt in range(2):
                        o = S2[j % 2][:, cols_at[kt][0]:cols_at[kt][1]]
                        k = kr[0:SHIFT_ROW + 2, c, j, kt * P:(kt + 1) * P]
                        if not causal:
                            last = t.matmul(o, k, qr[0:SHIFT_ROW + 2, c, j], start=True, stop=True)
                        else:
                            if kt == 0:
                                t.matmul(o[:, P:T], k, qr[0:SHIFT_ROW + 2, c, j, P:T], start=True, stop=True)
                            o = o[:, 0:P]
                            t.matmul(o, k, qr[0:SHIFT_ROW + 2, c, j, kt * P:(kt + 1) * P], start=True, stop=False)
                            last = t.matmul(o, m.identb[:, :], mask_cols, start=False, stop=True)
                    last.then_inc(s["col_scores"], 1)

                def turn_max(i, c, n):
                    pe.wait_ge(s["maxed"], n * QH + QH)
                    wait_past(pe, s["shift_lo"], n)
                    for qt in range(2):
                        last = t.transpose(MX[:, qt * P:(qt + 1) * P], mx[:, c % 2, qt], m.const("ident"))
                    last.then_inc(s["mx_t"], 1)

                def values(i, c, n):
                    pe.wait_ge(s["probs"], n * QH + QH)
                    pe.wait_ge(s["vals"], n + 1)
                    wait_past(pe, s["pv_sb"], n)
                    parts = [(0, (0, P), True, True), (0, (P, T), True, False), (1, (P, T), False, True)] if causal \
                        else [(0, (0, T), True, False), (1, (0, T), False, True)]
                    for kt, (q0, q1), first, final in parts:
                        at_q = cols_at[kt][0] + (q0 if not causal or kt == 0 else 0)
                        for j in range(QH):
                            last = t.matmul(PV[32 * j:32 * j + D + 1, q0:q1], vals[:, c % QUADS, kt, j, :],
                                            probs[:, c % 2, j, at_q:at_q + q1 - q0], start=first, stop=final)
                    last.then_inc(s["pv"], 1)

                def turn_heads(i, c, n):
                    pe.wait_ge(s["pv_sb"], n + 1)
                    wait_past(pe, s["otok"], n)
                    for qt in range(2):
                        last = t.transpose(OT[:, qt * P:(qt + 1) * P], pv_sb[:, c % 2, qt * P:(qt + 1) * P],
                                           m.const("ident"))
                    last.then_inc(s["ot_ps"], 1)

                def turn_all(b):
                    pe.wait_ge(s["otok"], (b + 1) * QUADS)
                    wait_past(pe, s["added"], b)
                    for qt in range(2):
                        last = t.transpose(FIN[:, qt * P:(qt + 1) * P], otok[:, qt].rearrange("p h d -> p (h d)"),
                                           m.const("ident"))
                    last.then_inc(s["otok_t"], 1)

                def project(b):
                    pe.wait_ge(s["ot"], b + 1)
                    for qt in range(2):
                        last = t.matmul(FIN[:, qt * P:(qt + 1) * P], ot[:, qt * P:(qt + 1) * P], Wo, start=True, stop=True)
                    last.then_inc(s["proj"], 1)

                def slot(i, c, n, live):
                    for j in range(QH):
                        if live(3):
                            row_scores(*at(i, c, 3), j)
                        if j == 0 and live(-2):
                            turn_heads(*at(i, c, -2))
                        if j == 1 and live(2):
                            turn_max(*at(i, c, 2))
                        if j == 2 and live(-1):
                            values(*at(i, c, -1))
                        col_scores(i, c, n, j)
                    if live(-QUADS) and c % QUADS == 2:
                        turn_all(batch(i, c) - 1)
                    if live(-QUADS) and c % QUADS == 3:
                        project(batch(i, c) - 1)

                for c in range(3):
                    for j in range(QH):
                        row_scores(0, c, c, j)
                    if c >= 1:
                        turn_max(0, c - 1, c - 1)
                quads(pe, slot)
                values(*END)
                turn_heads(*at(*END[:2], -1))
                turn_heads(*END)
                turn_all(B - 1)
                project(B - 1)

            @block.scalar
            def _(act):
                a = nc.scalar

                def exponential(i, c, n, j):
                    act.wait_ge(s["col_scores"], n * QH + j + 1)
                    w = cols_at[1][1]
                    a.activation(probs[:, c % 2, j, 0:w], S2[j % 2][:, 0:w], ACT.Exp, scale=SCALE).then_inc(s["probs"], 1)

                def copy_values(i, c, n):
                    act.wait_ge(s["pv"], n + 1)
                    wait_past(act, s["ot_ps"], n - 1)
                    a.activation(pv_sb[:, c % 2], PV, ACT.Copy).then_inc(s["pv_sb"], 1)

                def copy_heads(b):
                    act.wait_ge(s["otok_t"], b + 1)
                    a.activation(ot, FIN, ACT.Copy).then_inc(s["ot"], 1)

                def shift_high(i, c, n):
                    act.wait_ge(s["mx_t"], n + 1)
                    wait_past(act, shifted[c % 2], (i * QUADS + c // 2) * (16 * SHIFTS))
                    a.activation(shift[0:QH, c % 2, 0], MX, ACT.Copy).then_inc(s["shift_hi"], 1)

                def slot(i, c, n, live):
                    wait_past(act, s["pv"], n - 1)
                    exponential(i, c, n, 0)
                    if live(2):
                        shift_high(*at(i, c, 2))
                    exponential(i, c, n, 1)
                    if live(-1):
                        copy_values(*at(i, c, -1))
                    exponential(i, c, n, 2)
                    exponential(i, c, n, 3)
                    if live(-QUADS) and c % QUADS == 2:
                        copy_heads(batch(i, c) - 1)

                shift_high(0, 0, 0)
                shift_high(0, 1, 1)
                quads(act, slot)
                copy_values(*END)
                copy_heads(B - 1)

            @block.vector
            def _(dve):
                v = nc.vector

                def maximum(i, c, n, j):
                    if j == 0:
                        wait_past(dve, s["mx_t"], n - 1)
                    dve.wait_ge(s["row_scores"], n * QH + j + 1)
                    if causal:
                        for qt in range(2):
                            last = v.tensor_reduce(mx[:, c % 2, qt, j:j + 1], S1[j % 2][:, rows_at[qt][0]:rows_at[qt][1]],
                                                   AX.X, ALU.max)
                    else:
                        last = v.tensor_reduce(mx[:, c % 2, :, j], S1[j % 2].rearrange("p (q k) -> p q k", q=2),
                                               AX.X, ALU.max)
                    last.then_inc(s["maxed"], 1)

                def shift_low(i, c, n):
                    dve.wait_ge(s["shift_hi"], n + 1)
                    v.tensor_tensor(shift[0:QH, c % 2, 1], MX, shift[0:QH, c % 2, 0], ALU.subtract)\
                        .then_inc(s["shift_lo"], 1)

                o = OT.rearrange("p (q j r) -> p q j r", q=2, j=QH)

                def invert(i, c, n):
                    dve.wait_ge(s["ot_ps"], n + 1)
                    wait_past(dve, s["otok"], n)
                    v.reciprocal(rec, o[:, :, :, D]).then_inc(s["recip"], 1)

                def normalise(i, c, n):
                    q = c % QUADS
                    dve.wait_ge(s["recip"], n + 1)
                    if q == 0:
                        wait_past(dve, s["otok_t"], batch(i, c))
                    v.tensor_tensor(otok[:, :, QH * q:QH * q + QH, :], o[:, :, :, 0:D],
                                    rec.unsqueeze(3).to_broadcast([P, 2, QH, D]), ALU.mult).then_inc(s["otok"], 1)

                def add(b):
                    dve.wait_ge(s["proj"], b + 1)
                    o = out[:, bass.ds(b * 2, 2), :]
                    v.tensor_tensor(o, FIN.rearrange("p (t c) -> p t c", t=2), o, ALU.add).then_inc(s["added"], 1)

                def slot(i, c, n, live):
                    for j in range(QH):
                        if live(3):
                            maximum(*at(i, c, 3), j)
                        if j == 1 and live(-2):
                            invert(*at(i, c, -2))
                        if j == 2:
                            if live(2):
                                shift_low(*at(i, c, 2))
                            if live(-2):
                                normalise(*at(i, c, -2))
                    if live(-QUADS) and c % QUADS == 3:
                        add(batch(i, c) - 1)

                v.memset(kr[SHIFT_ROW:P], -1.0)
                v.memset(qr.bitcast(F32), 0.0).then_inc(s["zeroed"], 1)
                for c in range(3):
                    for j in range(QH):
                        maximum(0, c, c, j)
                    if c >= 1:
                        shift_low(0, c - 1, c - 1)
                quads(dve, slot)
                for quad in (at(*END[:2], -1), END):
                    invert(*quad)
                    normalise(*quad)
                add(B - 1)


class Routing:

    def __init__(self, m):
        at = [ARENA]

        def take(*shape):
            n = int(np.prod(shape))
            at[0] -= n
            flat = m.arena[:, at[0]:at[0] + n]
            return flat if len(shape) == 1 else flat.rearrange("p (t e) -> p t e", e=shape[1])
        self.logits = take(TILES, E)
        self.one = [take(TILES, E) for _ in range(2)]
        self.prob = [take(TILES) for _ in range(2)]
        self.top = [take(TILES) for _ in range(2)]
        self.weights = take(TILES, E)
        self.place = [take(TILES) for _ in range(2)]
        self.expert = take(SLOT_TILES)


def gate(nc, m, name, r, src, Wg, bias, z_keep, zt_keep):
    with ExitStack() as ctx:
        s = semaphores(nc, ctx, name, NORM + "zt_ps zt kept logit_ps logit_sb turned")
        take = m.layout()
        if zt_keep:
            take(TILES, P)
        else:
            take(TILES, 2, ROW)
        z = take(2, GT, P)
        zt = take(2, GN)
        lt = take(2, GN)
        psT = [m.ps[:, u, :] for u in range(2)]
        psL = [m.ps[0:E, 2 + u, :] for u in range(2)]
        psR = m.ps[:, 4, 0:TILES * E]

        def channels(n, u):
            return m.arena[:, bass.ds(n * GN, GN)] if zt_keep else zt[:, u]

        with nc.Block() as block:
            @block.gpsimd
            def _(pool):
                def body(i):
                    for u in range(2):
                        if z_keep is not None:
                            wait_past(pool, s["kept"], i * 2 + u - 1)
                        normed(nc, pool, m, s, i, u, src, None, z)
                loop(pool, GROUPS // 2, body)

            @block.tensor
            def _(pe):
                t = nc.tensor

                def part(i, u, live):
                    n = i * 2 + u
                    if live(2):
                        turned(nc, pe, m, s, n + 2, u, z, psT)
                    if live(1):
                        pe.wait_ge(s["zt"], n + 2)
                        wait_past(pe, s["logit_sb"], n)
                        t.matmul(psL[1 - u], Wg, channels(n + 1, 1 - u), start=True, stop=True).then_inc(s["logit_ps"], 1)
                    if live(0):
                        pe.wait_ge(s["logit_sb"], n + 1)
                        for k in range(GT):
                            last = t.matmul(psR[:, bass.ds((n * GT + k) * E, E)], lt[0:E, u, k * P:(k + 1) * P],
                                            m.const("ident")[0:E, 0:E], start=True, stop=True)
                        last.then_inc(s["turned"], 1)
                steps(pe, part, 2)

            @block.scalar
            def _(act):
                a = nc.scalar

                def part(i, u, live):
                    n = i * 2 + u
                    if live(2):
                        act.wait_ge(s["zt_ps"], n + 3)
                        wait_past(act, s["logit_ps"], n + 1)
                        a.activation(channels(n + 2, u), psT[u], ACT.Copy).then_inc(s["zt"], 1)
                        if not zt_keep:
                            for k in range(2):
                                last = a.activation(z_keep[:, tiles_of(n + 2), k, 0:P], z[:, u], ACT.Copy)
                            last.then_inc(s["kept"], 1)
                    if live(1) and not live(0):
                        norm_roots(nc, act, m, s, 1)
                    if live(1):
                        act.wait_ge(s["logit_ps"], n + 2)
                        wait_past(act, s["turned"], n)
                        a.activation(lt[0:E, 1 - u], psL[1 - u], ACT.Identity, bias=bias).then_inc(s["logit_sb"], 1)
                norm_roots(nc, act, m, s, 0)
                steps(act, part, 2)

            @block.vector
            def _(dve):
                v = nc.vector

                for half in range(2):
                    norm_stats(nc, dve, m, s, half, src)
                dve.wait_ge(s["turned"], GROUPS)
                v.tensor_copy(r.logits, psR.rearrange("p (t e) -> p t e", e=E))


def choose(nc, m, name, r, dispatch=None):
    with ExitStack() as ctx:
        s = semaphores(nc, ctx, name, "link gap exp chosen ranks counts")
        take = m.layout()
        take(TILES, 2, ROW)
        best, key, key_top, masked = take(TILES, E), take(TILES, E), take(TILES), take(TILES, E)
        gap, e_gap = take(TILES), take(TILES)
        ones, both = take(P), take(TILES, E)
        total, keep, upto = take(E, TILES), take(E, TILES), take(E, TILES)
        pos, count, tiles, ends, bases, one8 = take(TILES, E), take(E), take(E), take(E), take(E), take(E)
        whole = take(E).bitcast(I32)
        over, fexp, fpl = take(SLOT_TILES, E), take(SLOT_TILES), take(TILES)
        RANK, TOTAL = m.ps[:, 0, 0:TILES * E], m.ps[:, 1, 0:TILES * E]

        def along(x, n=E):
            return x.unsqueeze(2).to_broadcast([P, TILES, n])

        with nc.Block() as block:
            @block.vector
            def _(dve):
                v, done = nc.vector, [0]

                def link(ins):
                    done[0] += 1
                    ins.then_inc(s["link"], 1)
                    dve.wait_ge(s["link"], done[0])

                rev = m.const("rev").unsqueeze(1).to_broadcast([P, TILES, E])
                left = r.logits
                for c in range(2):
                    link(v.tensor_reduce(r.top[c], left, AX.X, ALU.max))
                    link(v.tensor_tensor(best, left, along(r.top[c]), ALU.is_equal))
                    link(v.tensor_tensor(key, best, rev, ALU.mult))
                    link(v.tensor_reduce(key_top, key, AX.X, ALU.max))
                    link(v.tensor_tensor(r.one[c], rev, along(key_top), ALU.is_equal))
                    if c == 0:
                        link(v.scalar_tensor_tensor(out=masked, in0=r.one[0], scalar=-3e38, in1=r.logits,
                                                    op0=ALU.mult, op1=ALU.add))
                        left = masked
                v.tensor_tensor(gap, r.top[1], r.top[0], ALU.subtract).then_inc(s["gap"], 1)
                if dispatch is not None:
                    v.memset(ones, 1.0)
                    v.tensor_tensor(both, r.one[0], r.one[1], ALU.add).then_inc(s["chosen"], 1)
                    v.memset(one8, 1.0)
                    link(v.memset(keep, 1.0))
                    link(v.memset(keep[:, :, 0:1], 0.0))
                dve.wait_ge(s["exp"], 1)
                link(v.tensor_scalar(gap, e_gap, 1.0, None, ALU.add))
                link(v.reciprocal(r.prob[0], gap))
                link(v.tensor_tensor(r.prob[1], r.prob[0], e_gap, ALU.mult))
                if dispatch is None:
                    link(v.tensor_tensor(best, r.one[0], along(r.prob[0]), ALU.mult))
                    link(v.tensor_tensor(key, r.one[1], along(r.prob[1]), ALU.mult))
                    link(v.tensor_tensor(r.weights, best, key, ALU.add))
                    return
                dve.wait_ge(s["counts"], 1)
                link(v.tensor_copy(total, TOTAL.rearrange("p (t e) -> p e t", e=E)))
                link(v.tensor_tensor_scan(upto.rearrange("p e t -> p (e t)"), keep.rearrange("p e t -> p (e t)"),
                                          total.rearrange("p e t -> p (e t)"), 0.0, ALU.mult, ALU.add))
                link(v.tensor_scalar(count, upto[:, :, TILES - 1], float(P - 1), None, ALU.add))
                link(v.tensor_copy(whole, count))
                link(v.tensor_scalar(whole, whole, 7, None, ALU.arith_shift_right))
                link(v.tensor_copy(tiles, whole))
                link(v.tensor_tensor_scan(ends, one8, tiles, 0.0, ALU.mult, ALU.add))
                link(v.tensor_tensor(bases, ends, tiles, ALU.subtract))
                link(v.tensor_scalar(bases, bases, float(P), None, ALU.mult))
                link(v.tensor_tensor(upto, upto, total, ALU.subtract))
                link(v.tensor_tensor(upto, upto, bases.unsqueeze(2).to_broadcast([P, E, TILES]), ALU.add))
                link(v.tensor_tensor(pos, RANK.rearrange("p (t e) -> p t e", e=E), upto.rearrange("p e t -> p t e"), ALU.add))
                for c in range(2):
                    link(v.tensor_tensor(key, r.one[c], pos, ALU.mult))
                    link(v.tensor_reduce(fpl, key, AX.X, ALU.add))
                    link(v.tensor_copy(r.place[c].bitcast(I32), fpl))
                    v.tensor_scalar(dispatch[:, :, c, P], r.prob[c], 0.5, None, ALU.mult)
                    link(v.tensor_scalar(fpl, m.const("token"), float(c * TOKENS), None, ALU.add))
                    link(v.tensor_copy(dispatch.bitcast(I32)[:, :, c, P + 1], fpl))
                link(v.tensor_tensor(over, m.const("slot").unsqueeze(2).to_broadcast([P, SLOT_TILES, E]),
                                     ends.unsqueeze(1).to_broadcast([P, SLOT_TILES, E]), ALU.is_ge))
                link(v.tensor_reduce(fexp, over, AX.X, ALU.add))
                link(v.tensor_scalar(fexp, fexp, float(E - 1), None, ALU.min))
                link(v.tensor_copy(r.expert.bitcast(I32), fexp))

            @block.scalar
            def _(act):
                act.wait_ge(s["gap"], 1)
                nc.scalar.activation(e_gap, gap, ACT.Exp).then_inc(s["exp"], 1)

            if dispatch is not None:
                @block.tensor
                def _(pe):
                    t = nc.tensor
                    pe.wait_ge(s["chosen"], 1)
                    flat = both.rearrange("p t e -> p (t e)")
                    t.matmul(RANK, m.const("before"), flat, start=True, stop=True)
                    t.matmul(TOTAL, ones, flat, start=True, stop=True).then_inc(s["counts"], 1)


def experts_dense(nc, m, name, r):
    with ExitStack() as ctx:
        s = semaphores(nc, ctx, name, "top rest mid low w_ps wt wide hidden relu scaled y base link done")
        take = m.layout()
        zt_all = take(TILES * P)
        w = take(TILES, P, dt=BF16)
        rest = take(TILES, E)
        wt = take(2, GN, dt=BF16)
        hid = take(2, GN)
        hs = take(2, CH, GN)
        psC = m.ps[:, 0, :]
        psB = [m.ps[:, 1 + u, :] for u in range(2)]
        psH = [m.ps[:, 3 + u, :] for u in range(2)]
        psY = [m.ps[:, 5 + u, :] for u in range(2)]
        with nc.Block() as block:
            @block.gpsimd
            def _(pool):
                g, top, mid, low = nc.gpsimd, w[:, :, 0:E], w[:, :, E:2 * E], w[:, :, 2 * E:3 * E]
                g.memset(w[:, :, :].rearrange("p t k -> p (t k)").bitcast(F32), 0.0).then_inc(s["top"], 1)
                pool.wait_ge(s["top"], 1)
                g.tensor_copy(top, r.weights).then_inc(s["top"], 1)
                pool.wait_ge(s["top"], 2)
                g.tensor_tensor(rest, r.weights, top, ALU.subtract).then_inc(s["rest"], 1)
                pool.wait_ge(s["rest"], 1)
                g.tensor_copy(mid, rest).then_inc(s["mid"], 1)
                pool.wait_ge(s["mid"], 1)
                g.tensor_tensor(low, rest, mid, ALU.subtract).then_inc(s["low"], 1)

            @block.tensor
            def _(pe):
                t = nc.tensor

                def products(n, u):
                    pe.wait_ge(s["scaled"], n * CH + CH)
                    wait_past(pe, s["done"], n - 1)
                    for k in range(GT):
                        for c in range(CH):
                            last = t.matmul(psY[u][:, k * P:(k + 1) * P], hs[:, u, c, k * P:(k + 1) * P],
                                            m.f_W2[:, c, :], start=(c == 0), stop=(c == CH - 1))
                    last.then_inc(s["y"], 1)

                pe.wait_ge(s["low"], 1)

                def part(i, u, live):
                    n, w_of = i * 2 + u + 1, 1 - u
                    if live(1):
                        wait_past(pe, s["wt"], n)
                        for k in range(GT):
                            last = t.matmul(psC[:, k * P:(k + 1) * P], w[:, n * GT + k, :], m.identb[:, :], start=True, stop=True)
                        last.then_inc(s["w_ps"], 1)
                    for c in range(CH):
                        if live(1):
                            wait_past(pe, s["relu"], n * CH + c - 1)
                            t.matmul(psH[c % 2], m.f_W1[:, c, :], zt_all[:, bass.ds(n * GN, GN)],
                                     start=True, stop=True).then_inc(s["hidden"], 1)
                            if c == 0:
                                pe.wait_ge(s["wt"], n + 1)
                            wait_past(pe, s["scaled"], n * CH + c - 1)
                            t.matmul(psB[c % 2], m.selb[:, c * P:(c + 1) * P], wt[:, w_of],
                                     start=True, stop=True).then_inc(s["wide"], 1)
                        if c == 1 and live(0):
                            products(n - 1, u)
                steps(pe, part, 1)

            @block.scalar
            def _(act):
                a = nc.scalar

                def body(i):
                    for u in range(2):
                        n = i * 2 + u
                        act.wait_ge(s["w_ps"], n + 1)
                        wait_past(act, s["wide"], (n - 1) * CH)
                        a.activation(wt[:, u], psC, ACT.Copy).then_inc(s["wt"], 1)
                        for c in range(CH):
                            act.wait_ge(s["hidden"], n * CH + c + 1)
                            wait_past(act, s["scaled"], n * CH + c - 1)
                            a.activation(hid[:, c % 2], psH[c % 2], ACT.Relu, bias=m.f_bh[:, c:c + 1]).then_inc(s["relu"], 1)
                loop(act, GROUPS // 2, body)

            @block.vector
            def _(dve):
                v = nc.vector

                def finish(n, u):
                    xs = m.x[:, tiles_of(n), :]
                    v.scalar_tensor_tensor(out=xs, in0=m.xi[:, tiles_of(n), :], scalar=0.5, in1=xs,
                                           op0=ALU.mult, op1=ALU.add).then_inc(s["base"], 1)
                    dve.wait_ge(s["y"], n + 1)
                    dve.wait_ge(s["base"], n + 1)
                    v.scalar_tensor_tensor(out=xs, in0=psY[u].rearrange("p (t c) -> p t c", t=GT), scalar=0.5, in1=xs,
                                           op0=ALU.mult, op1=ALU.add).then_inc(s["done"], 1)

                def body(i):
                    for u in range(2):
                        n = i * 2 + u
                        for c in range(CH):
                            dve.wait_ge(s["relu"], n * CH + c + 1)
                            dve.wait_ge(s["wide"], n * CH + c + 1)
                            if c == 0:
                                wait_past(dve, s["y"], n - 1)
                            v.tensor_tensor(hs[:, u, c], hid[:, c % 2], psB[c % 2], ALU.mult).then_inc(s["scaled"], 1)
                            if c == 2 and not (isinstance(n, int) and n == 0):
                                finish(n - 1, 1 - u)
                loop(dve, GROUPS // 2, body)
                finish(GROUPS - 1, 1)


def scatter(nc, m, name, r, rows, slots):
    with ExitStack() as ctx:
        s = semaphores(nc, ctx, name, "sent")
        with nc.Block() as block:
            @block.gpsimd
            def _(pool):
                pool.wait_ge(m.late, 16 * LATE)
                for t in range(TILES):
                    for c in range(2):
                        pool.indirect_dma_start(
                            slots, bass.IndirectOffsetOnAxis(ap=r.place[c].bitcast(I32)[:, t:t + 1], axis=0),
                            rows[:, t, c, :], None).then_inc(s["sent"], 16)
                pool.wait_ge(s["sent"], 2 * TILES * 16)


def experts_routed(nc, m, name, r, slots, results):
    with ExitStack() as ctx:
        s = semaphores(nc, ctx, name, "load0 load1 load2 load3 load4 load5 load6 load7 zt_ps zt up x1 gated gated_t gated_sb mix act act_t act_sb down out "
                       "sent0 sent1 taken")
        take = m.layout()
        rows = take(RING, ROW)
        zt, x1, gated, gated_t = take(2, P), take(2, F1), take(2, F1), take(2, F1)
        acts, acts_t, out = take(2, F1), take(2, F1), take(2, P)
        psZ, psU = m.ps[:, 0, 0:P], m.ps[:, 1, :]
        psG, psM = m.ps[:, 2, 0:F1], m.ps[:, 3, 0:F1]
        psA, psD = m.ps[:, 4, 0:F1], m.ps[:, 5, 0:P]

        def each(eng, parts, reach):
            n = SLOT_TILES // RING
            for u in range(RING):
                parts(u, u, lambda d, t=u: t - d >= 0)
            with eng.Fori(1, n) as i:
                for u in range(RING):
                    parts(i * RING + u, u, lambda d: True)
            for t in range(SLOT_TILES, SLOT_TILES + reach):
                parts(t, t % RING, lambda d, t=t: t - d < SLOT_TILES)

        def sent_count(t, u, back):
            if isinstance(t, int):
                return (t - back) // 2 * 16 + 16 if t >= back else 0
            return (t - u) * 8 + (u // 2 - back // 2 + 1) * 16

        with nc.Block() as block:
            @block.sync
            def _(sp):
                def parts(t, u, live):
                    if live(0):
                        wait_past(sp, s[f"sent{u % 2}"], sent_count(t, u, RING))
                        sp.dma_start(rows[:, u], slots[bass.ds(t * P, P), :]).then_inc(s[f"load{u}"], 16)
                each(sp, parts, 0)

            @block.tensor
            def _(pe):
                tn = nc.tensor
                ident = m.const("ident")

                def turn(ps, src, n):
                    for k in range(n):
                        last = tn.transpose(ps[:, k * P:(k + 1) * P], src[:, k * P:(k + 1) * P], ident)
                    return last

                held = [tn.alloc_register(f"{name}_expert{u}") for u in range(RING)]

                def fetch_expert(t, u):
                    tn.reg_load(held[u], r.expert.bitcast(I32)[0:1, bass.ds(t, 1)])

                def product(ps, lhs, e, weights, bias_at, bias_n, sem):
                    for k, w in enumerate(weights):
                        tn.matmul(ps, lhs[:, k * P:(k + 1) * P], w[:, bass.ds(e, 1), :].rearrange("p o f -> p (o f)"),
                                  start=(k == 0), stop=False)
                    tn.matmul(ps, m.ones3[:, :],
                              m.bias3[:, bass.ds(e, 1), bias_at:bias_at + bias_n].rearrange("p o f -> p (o f)"),
                              start=False, stop=True).then_inc(sem, 1)

                def turn_rows(t, u):
                    pe.wait_ge(s[f"load{u}"], (t - u) * 2 + 16)
                    wait_past(pe, s["zt"], t)
                    turn(psZ, rows[:, u, 0:P], 1).then_inc(s["zt_ps"], 1)

                def parts(t, u, live):
                    es = {d: tn.snap(held[(u - d) % RING], min_val=0, max_val=E - 1) for d in (0, 1, 2) if live(d)}
                    if live(1):
                        pe.wait_ge(s["gated"], t)
                        wait_past(pe, s["gated_sb"], t - 1)
                        turn(psG, gated[:, (u - 1) % 2], 2).then_inc(s["gated_t"], 1)
                    if live(0):
                        pe.wait_ge(s["zt"], t + 1)
                        wait_past(pe, s["gated"], t)
                        product(psU, zt[:, u % 2], es[0], [m.w12], 0, 2 * F1, s["up"])
                    if live(-1):
                        fetch_expert(t + 1, (u + 1) % RING)
                    if live(2):
                        pe.wait_ge(s["act"], t - 1)
                        wait_past(pe, s["act_sb"], t - 2)
                        turn(psA, acts[:, u % 2], 2).then_inc(s["act_t"], 1)
                    if live(-1):
                        turn_rows(t + 1, (u + 1) % RING)
                    if live(1):
                        pe.wait_ge(s["gated_sb"], t)
                        wait_past(pe, s["act"], t - 1)
                        product(psM, gated_t[:, (u - 1) % 2], es[1], [m.wg[:, 0], m.wg[:, 1]], 2 * F1, F1, s["mix"])
                    if live(2):
                        pe.wait_ge(s["act_sb"], t - 1)
                        wait_past(pe, s["out"], t - 2)
                        product(psD, acts_t[:, u % 2], es[2], [m.w3[:, 0], m.w3[:, 1]], 3 * F1, P, s["down"])

                fetch_expert(0, 0)
                turn_rows(0, 0)
                n = SLOT_TILES // RING
                for u in range(RING):
                    parts(u, u, lambda d, t=u: t - d >= 0)
                with pe.Fori(1, n - 1) as i:
                    for u in range(RING):
                        parts(i * RING + u, u, lambda d: True)
                for t in range(SLOT_TILES - RING, SLOT_TILES + 2):
                    parts(t, t % RING, lambda d, t=t: t - d < SLOT_TILES)

            @block.scalar
            def _(act):
                a = nc.scalar

                def take_rows(t, u):
                    act.wait_ge(s["zt_ps"], t + 1)
                    wait_past(act, s["up"], t - 1)
                    a.activation(zt[:, u % 2], psZ, ACT.Copy).then_inc(s["zt"], 1)

                def parts(t, u, live):
                    if live(0):
                        act.wait_ge(s["up"], t + 1)
                        wait_past(act, s["gated"], t - 1)
                        a.activation(x1[:, u % 2], psU[:, 0:F1], ACT.Copy).then_inc(s["x1"], 1)
                    if live(-1):
                        take_rows(t + 1, (u + 1) % RING)
                    if live(1):
                        act.wait_ge(s["mix"], t)
                        wait_past(act, s["act_t"], t - 2)
                        a.activation(acts[:, (u - 1) % 2], psM, ACT.Silu).then_inc(s["act"], 1)
                    if live(2):
                        act.wait_ge(s["down"], t - 1)
                        wait_past(act, s[f"sent{u % 2}"], sent_count(t, u, 4))
                        a.activation(out[:, u % 2], psD, ACT.Copy, scale=rows[:, (u - 2) % RING, P:P + 1]).then_inc(s["out"], 1)

                take_rows(0, 0)
                n = SLOT_TILES // RING
                for u in range(RING):
                    parts(u, u, lambda d, t=u: t - d >= 0)
                with act.Fori(1, n - 1) as i:
                    for u in range(RING):
                        parts(i * RING + u, u, lambda d: True)
                for t in range(SLOT_TILES - RING, SLOT_TILES + 2):
                    parts(t, t % RING, lambda d, t=t: t - d < SLOT_TILES)

            @block.vector
            def _(dve):
                v = nc.vector

                def parts(t, u, live):
                    if live(1):
                        dve.wait_ge(s["gated_t"], t)
                        wait_past(dve, s["mix"], t - 2)
                        v.tensor_copy(gated_t[:, (u - 1) % 2], psG).then_inc(s["gated_sb"], 1)
                    if live(0):
                        dve.wait_ge(s["x1"], t + 1)
                        wait_past(dve, s["gated_t"], t - 1)
                        v.tensor_tensor(gated[:, u % 2], x1[:, u % 2], psU[:, F1:2 * F1], ALU.mult).then_inc(s["gated"], 1)
                    if live(2):
                        dve.wait_ge(s["act_t"], t - 1)
                        wait_past(dve, s["down"], t - 3)
                        v.tensor_copy(acts_t[:, u % 2], psA).then_inc(s["act_sb"], 1)
                each(dve, parts, 2)

            @block.gpsimd
            def _(pool):
                last_row = nc.gpsimd.to_reg(2 * TOKENS - 1)

                def parts(t, u, live):
                    if live(0):
                        pool.wait_ge(s["out"], t + 1)
                        pool.sem_inc(s["taken"], 1)
                        pool.indirect_dma_start(
                            results, bass.IndirectOffsetOnAxis(ap=rows.bitcast(I32)[:, u, P + 1:P + 2], axis=0),
                            out[:, u % 2], None, bounds_check=last_row, oob_is_err=False).then_inc(s[f"sent{u % 2}"], 16)
                each(pool, parts, 0)
                for k in range(2):
                    pool.wait_ge(s[f"sent{k}"], SLOT_TILES // 2 * 16)


def combine(nc, m, name, results):
    with ExitStack() as ctx:
        s = semaphores(nc, ctx, name, "loaded0 loaded1 added")
        take = m.layout()
        got = take(2, GT * 2, P)
        half = results.rearrange("(c t p) d -> c p t d", c=2, p=P)
        with nc.Block() as block:
            @block.sync
            def _(sp):
                def body(i):
                    for c in range(2):
                        wait_past(sp, s["added"], i * 2 + c - 1)
                        sp.dma_start(got[:, c], half[c][:, bass.ds(i * 8, 8), :]).then_inc(s[f"loaded{c}"], 16)
                loop(sp, TILES // 8, body)

            @block.vector
            def _(dve):
                def body(i):
                    for c in range(2):
                        dve.wait_ge(s[f"loaded{c}"], i * 16 + 16)
                        wait_past(dve, s["added"], i * 2 + c)
                        xs = m.x[:, bass.ds(i * 8, 8), :]
                        nc.vector.tensor_tensor(xs, xs, got[:, c], ALU.add).then_inc(s["added"], 1)
                loop(dve, TILES // 8, body)


def state_mix(nc, m, name):
    with ExitStack() as ctx:
        s = semaphores(nc, ctx, name, NORM + "zt_ps zt q_ps v_ps g_ps silu vt state y y_ps yt")
        take = m.layout()
        gates = take(TILES * P)
        z, zt = take(2, GT, P), take(2, GN)
        vt, state, y = take(2, GN), take(2, GN), take(2, GN)
        psT = [m.ps[:, u, :] for u in range(2)]
        psQ, psV, psG = m.ps[:, 2, :], m.ps[:, 3, :], m.ps[:, 4, :]
        psY = [m.ps[:, 5 + u, :] for u in range(2)]
        decay = m.col("s_decay").to_broadcast([P, T])
        with nc.Block() as block:
            @block.gpsimd
            def _(pool):
                loop(pool, GROUPS // 2, lambda i: [normed(nc, pool, m, s, i, u, m.x, None, z) for u in range(2)])

            @block.tensor
            def _(pe):
                t = nc.tensor

                def part(i, u, live):
                    n, w = i * 2 + u, 1 - u
                    if live(2):
                        turned(nc, pe, m, s, n + 2, u, z, psT)
                    if live(1):
                        pe.wait_ge(s["zt"], n + 2)
                        wait_past(pe, s["vt"], n + 1)
                        t.matmul(psV, m.mat("s_WvT"), zt[:, w], start=True, stop=True).then_inc(s["v_ps"], 1)
                        wait_past(pe, s["silu"], n + 1)
                        t.matmul(psG, m.mat("s_WgT"), zt[:, w], start=True, stop=True).then_inc(s["g_ps"], 1)
                        wait_past(pe, s["y"], n + 1)
                        t.matmul(psQ, m.mat("s_WqT"), zt[:, w], start=True, stop=True).then_inc(s["q_ps"], 1)
                    if live(0):
                        pe.wait_ge(s["y"], n + 1)
                        wait_past(pe, s["yt"], n - 1)
                        for k in range(GT):
                            last = t.transpose(psY[u][:, k * P:(k + 1) * P], y[:, u, k * P:(k + 1) * P], m.const("ident"))
                        last.then_inc(s["y_ps"], 1)
                steps(pe, part, 2)

            @block.scalar
            def _(act):
                a = nc.scalar

                def part(i, u, live):
                    n, w = i * 2 + u, 1 - u
                    if live(2):
                        act.wait_ge(s["zt_ps"], n + 3)
                        wait_past(act, s["q_ps"], n + 1)
                        a.activation(zt[:, u], psT[u], ACT.Copy).then_inc(s["zt"], 1)
                    if live(1) and not live(0):
                        norm_roots(nc, act, m, s, 1)
                    if live(1):
                        act.wait_ge(s["v_ps"], n + 2)
                        wait_past(act, s["state"], 2 * n)
                        a.activation(vt[:, w], psV, ACT.Copy).then_inc(s["vt"], 1)
                        act.wait_ge(s["g_ps"], n + 2)
                        a.activation(gates[:, bass.ds((n + 1) * GN, GN)], psG, ACT.Silu).then_inc(s["silu"], 1)
                    if live(0):
                        act.wait_ge(s["y_ps"], n + 1)
                        a.activation(m.xi[:, tiles_of(n), :], psY[u].rearrange("p (t c) -> p t c", t=GT), ACT.Copy)\
                            .then_inc(s["yt"], 1)
                norm_roots(nc, act, m, s, 0)
                steps(act, part, 2)

            @block.vector
            def _(dve):
                v = nc.vector

                def part(i, u, live):
                    n = i * 2 + u
                    dve.wait_ge(s["vt"], n + 1)
                    for b in range(2):
                        v.tensor_tensor_scan(state[:, u, b * T:(b + 1) * T], decay, vt[:, u, b * T:(b + 1) * T],
                                             0.0, ALU.mult, ALU.add).then_inc(s["state"], 1)
                    dve.wait_ge(s["q_ps"], n + 1)
                    dve.wait_ge(s["state"], 2 * n + 2)
                    wait_past(dve, s["y_ps"], n - 1)
                    v.tensor_tensor(y[:, u], psQ, state[:, u], ALU.mult).then_inc(s["y"], 1)
                for half in range(2):
                    norm_stats(nc, dve, m, s, half, m.x)
                steps(dve, part)


def state_out(nc, m, name):
    with ExitStack() as ctx:
        s = semaphores(nc, ctx, name, NORM + "zt_ps zt mixed y_ps added")
        take = m.layout()
        gates = take(TILES * P)
        z, zt, y = take(2, GT, P), take(2, GN), take(2, GN)
        psT = [m.ps[:, u, :] for u in range(2)]
        psY = [m.ps[:, 2 + u, :] for u in range(2)]
        with nc.Block() as block:
            @block.gpsimd
            def _(pool):
                loop(pool, GROUPS // 2, lambda i: [normed(nc, pool, m, s, i, u, m.xi, None, z) for u in range(2)])

            @block.tensor
            def _(pe):
                t = nc.tensor

                def part(i, u, live):
                    n = i * 2 + u
                    if live(1):
                        turned(nc, pe, m, s, n + 1, 1 - u, z, psT)
                    if live(0):
                        pe.wait_ge(s["mixed"], n + 1)
                        wait_past(pe, s["added"], n - 1)
                        for k in range(GT):
                            last = t.matmul(psY[u][:, k * P:(k + 1) * P], y[:, u, k * P:(k + 1) * P],
                                            m.mat("s_WoT"), start=True, stop=True)
                        last.then_inc(s["y_ps"], 1)
                steps(pe, part, 1)

            @block.scalar
            def _(act):
                def part(i, u, live):
                    n = i * 2 + u
                    act.wait_ge(s["zt_ps"], n + 1)
                    wait_past(act, s["mixed"], n - 1)
                    nc.scalar.activation(zt[:, u], psT[u], ACT.Identity, bias=m.col("s_beta"), scale=m.col("s_gamma"))\
                        .then_inc(s["zt"], 1)

                    if isinstance(n, int) and n == 0:
                        norm_roots(nc, act, m, s, 1)
                norm_roots(nc, act, m, s, 0)
                steps(act, part)

            @block.vector
            def _(dve):
                v = nc.vector

                def part(i, u, live):
                    n = i * 2 + u
                    if live(1):
                        w = 1 - u
                        dve.wait_ge(s["zt"], n + 2)
                        wait_past(dve, s["y_ps"], n)
                        v.tensor_tensor(y[:, w], zt[:, w], gates[:, bass.ds((n + 1) * GN, GN)], ALU.mult)\
                            .then_inc(s["mixed"], 1)
                    if live(0):
                        dve.wait_ge(s["y_ps"], n + 1)
                        xs = m.x[:, tiles_of(n), :]
                        v.tensor_tensor(xs, psY[u].rearrange("p (t c) -> p t c", t=GT), xs, ALU.add)\
                            .then_inc(s["added"], 1)
                for half in range(2):
                    norm_stats(nc, dve, m, s, half, m.xi)
                steps(dve, part, 1)


def first_ffn(nc, m, dram, name):
    attention_operands(nc, m, name + "_qkv", (m.mat("f_Wq"), m.mat("f_Wk"), m.mat("f_Wv")),
                       (m.f_bqk[:, 0:1], m.f_bqk[:, 1:2]), m.f_bv[:, :], dram, twice=True)
    attention(nc, m, name + "_att", m.mat("f_Wo"), dram, False, m.xi)
    r = Routing(m)
    gate(nc, m, name + "_gate", r, m.xi, m.f_Wg[:, :], m.f_bg[:, :], None, True)
    choose(nc, m, name + "_choose", r)
    experts_dense(nc, m, name + "_experts", r)


def first_attention(nc, m, dram, name):
    attention_operands(nc, m, name + "_qkv", (m.mat("a_WqT"), m.mat("a_Wk"), m.mat("a_Wv")),
                       (m.col("a_bq"), m.col("a_bk")), m.row("a_bv"), dram, twice=False)
    attention(nc, m, name + "_att", m.mat("a_Wo"), dram, True, m.x)


def second_ffn(nc, m, dram, name, which):
    r = Routing(m)
    rows = m.arena[:, 0:TILES * 2 * ROW].rearrange("p (t c w) -> p t c w", c=2, w=ROW)
    gate(nc, m, name + "_gate", r, m.x, m.m_Wg[:, :], m.col("m_gate_b")[0:E, :], rows, False)
    choose(nc, m, name + "_choose", r, dispatch=rows)
    scatter(nc, m, name + "_scatter", r, rows, dram["slots"][which])
    experts_routed(nc, m, name + "_experts", r, dram["slots"][which], dram["results"][which])
    combine(nc, m, name + "_combine", dram["results"][which])


def second_attention(nc, m, name):
    state_mix(nc, m, name + "_mix")
    state_out(nc, m, name + "_out")


def build(nc, dram, stages=6):
    with ExitStack() as ctx:
        m = Memory(nc, ctx)
        setup(nc, m, dram)
        steps = [lambda: first_ffn(nc, m, dram, "f1"), lambda: first_attention(nc, m, dram, "a1"),
                 lambda: first_ffn(nc, m, dram, "f2"), lambda: second_ffn(nc, m, dram, "g1", 0),
                 lambda: second_attention(nc, m, "a2"), lambda: second_ffn(nc, m, dram, "g2", 1)]
        for step in steps[:stages]:
            step()
        dump(nc, m, dram, m.x)


def dump(nc, m, dram, src):
    with ExitStack() as ctx:
        s = semaphores(nc, ctx, "out", "stored")
        with nc.Block() as block:
            @block.sync
            def _(sp):
                sp.dma_start(dram["out"].rearrange("(t p) c -> p t c", p=P), src[:, :, :]).then_inc(s["stored"], 16)
                sp.wait_ge(s["stored"], 16)


def kernel(**inputs):
    import numpy as _np
    import concourse.bacc as _bacc
    from concourse import mybir as _mybir
    from concourse.bass_utils import run_bass_kernel_spmd as _run

    a = {k: _np.ascontiguousarray(v) for k, v in inputs.items()}
    f, q, r, e = "L0_ffn_", "L0_attn_", "L1_attn_", "L1_ffn_"
    cols = {
        "f_g1": a[f + "g1"], "f_b1": a[f + "b1"], "f_g2": a[f + "g2"], "f_b2": a[f + "b2"],
        "a_bq": a[q + "bq"], "a_bk": _np.tile(a[q + "bk"], H),
        "s_gamma": a[r + "ln_gamma"], "s_beta": a[r + "ln_beta"], "s_decay": _np.repeat(a[r + "decay"], D),
        "m_gate_b": _np.tile(a[e + "gate_b"], P // E),
    }
    arrays = {
        "x": a[q + "x"].reshape(TOKENS, P),
        "consts": _np.concatenate(list(CONST.values()), 1),
        "cols": _np.ascontiguousarray(_np.stack([cols[n] for n in COLS], 1)),
        "rows": _np.concatenate([_np.tile(a[q + "bv"], H), a[q + "bo"]])[None, :],
        "f_Wq": a[f + "Wq"], "f_Wk": a[f + "Wk"], "f_Wv": a[f + "Wv"], "f_Wo": a[f + "Wo"],
        "f_Wg": a[f + "Wg"], "f_W1": a[f + "W1"], "f_W2": a[f + "W2"],
        "a_WqT": a[q + "Wq"].T, "a_Wk": a[q + "Wk"], "a_Wv": a[q + "Wv"], "a_Wo": a[q + "Wo"],
        "s_WqT": a[r + "Wq"].T, "s_WvT": a[r + "Wv"].T, "s_WgT": a[r + "Wg"].T, "s_WoT": a[r + "Wo"].T,
        "m_Wg": a[e + "gate_w"], "m_w1": a[e + "w1"], "m_w2": a[e + "w2"], "m_wg": a[e + "wg"], "m_w3": a[e + "w3"],
        "m_biases": _np.concatenate([a[e + "b1"], a[e + "b2"], a[e + "bg"], a[e + "b3"]], 1),
    }
    arrays = {"in_" + k: _np.ascontiguousarray(v) for k, v in arrays.items()}
    nc = _bacc.Bacc("TRN2", target_bir_lowering=False, num_devices=1)
    dram = {k[3:]: nc.dram_tensor(k, v.shape, _mybir.dt.from_np(v.dtype), kind="ExternalInput").ap()
            for k, v in arrays.items()}
    dram["out"] = nc.dram_tensor("out", (TOKENS, P), F32, kind="ExternalOutput").ap()
    dram["q_parts"] = nc.dram_tensor("q_parts", (H, 3, D, TOKENS), BF16, kind="Internal").ap()
    dram["k_parts"] = nc.dram_tensor("k_parts", (H, len(PART_K), D, TOKENS), BF16, kind="Internal").ap()
    dram["slots"] = [nc.dram_tensor(f"slots{i}", (SLOTS, ROW), F32, kind="Internal").ap() for i in range(2)]
    dram["results"] = [nc.dram_tensor(f"results{i}", (2 * TOKENS, P), F32, kind="Internal").ap() for i in range(2)]
    build(nc, dram)
    got = _run(nc, [arrays], core_ids=[0])
    return got.results[0]["out"].reshape(B, T, P)
```
